# Optimizing a Trainium2 kernel written in Bass

```python
import numpy as np
import jax
import jax.numpy as jnp

def _softmax(x, axis=-1):
    return jax.nn.softmax(x, axis=axis)

def _gelu(x):
    return jax.nn.gelu(x, approximate=True)

def _silu(x):
    return jax.nn.silu(x)

def _sigmoid(x):
    return jax.nn.sigmoid(x)

def _layernorm(x, axis=-1, eps=1e-05):
    m = jnp.mean(x, axis=axis, keepdims=True)
    v = jnp.var(x, axis=axis, keepdims=True)
    return (x - m) / jnp.sqrt(v + eps)

def _scatter_add(tgt, idx, src, axis=0):
    return tgt.at[idx].add(src)

def _segment_sum(src, seg, n):
    return jax.ops.segment_sum(src, seg, n)
kernel_name = 'mk_macaron_d1_jaxref_r4_c984bd'

def setup_inputs(seed: int=0):
    np.random.seed(seed)
    _w = jnp.asarray

    def _L0_attn_setup():
        import jax, jax.numpy as jnp
        import numpy as np
        B, T, C, H = (8, 512, 256, 16)
        S = C // H
        LN_EPS = 1e-05
        key = jax.random.key(seed)
        ks = jax.random.split(key, 12)
        w = lambda k: jax.random.normal(k, (C, C), dtype=jnp.float32) * 0.02
        return {'x': jax.random.normal(ks[0], (B, T, C), dtype=jnp.float32), 'time_mix_k': jax.random.uniform(ks[1], (1, 1, C), dtype=jnp.float32), 'time_mix_v': jax.random.uniform(ks[2], (1, 1, C), dtype=jnp.float32), 'time_mix_r': jax.random.uniform(ks[3], (1, 1, C), dtype=jnp.float32), 'time_decay': -jax.random.uniform(ks[4], (H, S), minval=0.1, maxval=5.0, dtype=jnp.float32), 'time_first': jax.random.uniform(ks[5], (H, S), dtype=jnp.float32), 'Wk': w(ks[6]), 'Wv': w(ks[7]), 'Wr': w(ks[8]), 'Wo': w(ks[9]), 'ln_g': jnp.ones((C,), jnp.float32), 'ln_b': jnp.zeros((C,), jnp.float32)}
    _L0_attn_in = _L0_attn_setup()

    def _L0_ffn_setup():
        import jax, jax.numpy as jnp
        import numpy as np
        H = 256
        I = 128
        E = 8
        TOP_K = 2
        N_SHARED = 2
        SHARED_I = I * N_SHARED
        SCALE = 2.5
        NORM_TOPK = True
        B, S = (2, 256)

        def _swiglu(x, wg, wu, wd):
            g = x @ wg.T
            u = x @ wu.T
            return jax.nn.silu(g) * u @ wd.T
        key = jax.random.key(seed)
        ks = jax.random.split(key, 8)
        std = 0.02
        return {'hidden_states': jax.random.normal(ks[0], (B, S, H), jnp.float32), 'gate_weight': jax.random.normal(ks[1], (E, H), jnp.float32) * std, 'w_gate': jax.random.normal(ks[2], (E, I, H), jnp.float32) * std, 'w_up': jax.random.normal(ks[3], (E, I, H), jnp.float32) * std, 'w_down': jax.random.normal(ks[4], (E, H, I), jnp.float32) * std, 'ws_gate': jax.random.normal(ks[5], (SHARED_I, H), jnp.float32) * std, 'ws_up': jax.random.normal(ks[6], (SHARED_I, H), jnp.float32) * std, 'ws_down': jax.random.normal(ks[7], (H, SHARED_I), jnp.float32) * std}
    _L0_ffn_in = _L0_ffn_setup()
    _d = {'L0_attn_x': _L0_attn_in['x'], 'L0_attn_time_mix_k': _L0_attn_in['time_mix_k'], 'L0_attn_time_mix_v': _L0_attn_in['time_mix_v'], 'L0_attn_time_mix_r': _L0_attn_in['time_mix_r'], 'L0_attn_time_decay': _L0_attn_in['time_decay'], 'L0_attn_time_first': _L0_attn_in['time_first'], 'L0_attn_Wk': _L0_attn_in['Wk'], 'L0_attn_Wv': _L0_attn_in['Wv'], 'L0_attn_Wr': _L0_attn_in['Wr'], 'L0_attn_Wo': _L0_attn_in['Wo'], 'L0_attn_ln_g': _L0_attn_in['ln_g'], 'L0_attn_ln_b': _L0_attn_in['ln_b'], 'L0_ffn_gate_weight': _L0_ffn_in['gate_weight'], 'L0_ffn_w_gate': _L0_ffn_in['w_gate'], 'L0_ffn_w_up': _L0_ffn_in['w_up'], 'L0_ffn_w_down': _L0_ffn_in['w_down'], 'L0_ffn_ws_gate': _L0_ffn_in['ws_gate'], 'L0_ffn_ws_up': _L0_ffn_in['ws_up'], 'L0_ffn_ws_down': _L0_ffn_in['ws_down']}
    _x0 = _d['L0_attn_x']
    _d['L0_attn_x'] = jax.random.normal(jax.random.fold_in(jax.random.key(seed), 1), (16, 512, 256), dtype=_x0.dtype)
    del _x0
    return _d

def reference(L0_attn_x, L0_attn_time_mix_k, L0_attn_time_mix_v, L0_attn_time_mix_r, L0_attn_time_decay, L0_attn_time_first, L0_attn_Wk, L0_attn_Wv, L0_attn_Wr, L0_attn_Wo, L0_attn_ln_g, L0_attn_ln_b, L0_ffn_gate_weight, L0_ffn_w_gate, L0_ffn_w_up, L0_ffn_w_down, L0_ffn_ws_gate, L0_ffn_ws_up, L0_ffn_ws_down):

    def _L0_attn_ref(x, time_mix_k, time_mix_v, time_mix_r, time_decay, time_first, Wk, Wv, Wr, Wo, ln_g, ln_b):
        import jax, jax.numpy as jnp
        import numpy as np
        B, T, C, H = (8, 512, 256, 16)
        S = C // H
        LN_EPS = 1e-05
        Bx, Tx, Cx = x.shape
        xx = jnp.pad(x, ((0, 0), (1, 0), (0, 0)))[:, :-1]
        xk = x * time_mix_k + xx * (1 - time_mix_k)
        xv = x * time_mix_v + xx * (1 - time_mix_v)
        xr = x * time_mix_r + xx * (1 - time_mix_r)
        proj = lambda z, W: jnp.einsum('btc,dc->btd', z, W).reshape(Bx, Tx, H, S)
        k = proj(xk, Wk)
        v = proj(xv, Wv)
        r = proj(xr, Wr)
        kv = k * v
        decay = jnp.exp(time_decay)

        def step(state, inp):
            kv_t, r_t = inp
            state = kv_t + decay * state
            o = r_t * (time_first * kv_t + state)
            return (state, o)
        kvT = jnp.swapaxes(kv, 0, 1)
        rT = jnp.swapaxes(r, 0, 1)
        _, outT = jax.lax.scan(step, jnp.zeros((Bx, H, S), x.dtype), (kvT, rT))
        out = jnp.swapaxes(outT, 0, 1).reshape(Bx, Tx, Cx)
        mu = out.mean(-1, keepdims=True)
        var = out.var(-1, keepdims=True)
        out = (out - mu) / jnp.sqrt(var + LN_EPS) * ln_g + ln_b
        return jnp.einsum('btc,dc->btd', out, Wo)

    def _L0_ffn_ref(hidden_states, gate_weight, w_gate, w_up, w_down, ws_gate, ws_up, ws_down):
        import jax, jax.numpy as jnp
        import numpy as np
        H = 256
        I = 128
        E = 8
        TOP_K = 2
        N_SHARED = 2
        SHARED_I = I * N_SHARED
        SCALE = 2.5
        NORM_TOPK = True
        B, S = (2, 256)

        def _swiglu(x, wg, wu, wd):
            g = x @ wg.T
            u = x @ wu.T
            return jax.nn.silu(g) * u @ wd.T
        b, s, h = hidden_states.shape
        x = hidden_states.reshape(-1, h)
        shared_out = _swiglu(x, ws_gate, ws_up, ws_down)
        logits = x.astype(jnp.float32) @ gate_weight.astype(jnp.float32).T
        scores = jax.nn.sigmoid(logits)
        topk_w, topk_idx = jax.lax.top_k(scores, TOP_K)
        if TOP_K > 1 and NORM_TOPK:
            topk_w = topk_w / (topk_w.sum(-1, keepdims=True) + 1e-20)
        topk_w = topk_w * SCALE
        onehot = jax.nn.one_hot(topk_idx, E, dtype=topk_w.dtype)
        combine = jnp.einsum('tk,tke->te', topk_w, onehot)
        g = jnp.einsum('th,eih->tei', x, w_gate)
        u = jnp.einsum('th,eih->tei', x, w_up)
        hmid = jax.nn.silu(g) * u
        y = jnp.einsum('tei,ehi->teh', hmid, w_down)
        routed_out = jnp.einsum('te,teh->th', combine, y)
        out = (routed_out + shared_out).reshape(b, s, h)
        return out
    x = L0_attn_x
    x = x + 0.5 * _L0_ffn_ref(_layernorm(x, axis=-1), L0_ffn_gate_weight, L0_ffn_w_gate, L0_ffn_w_up, L0_ffn_w_down, L0_ffn_ws_gate, L0_ffn_ws_up, L0_ffn_ws_down)
    x = x + _L0_attn_ref(_layernorm(x, axis=-1), L0_attn_time_mix_k, L0_attn_time_mix_v, L0_attn_time_mix_r, L0_attn_time_decay, L0_attn_time_first, L0_attn_Wk, L0_attn_Wv, L0_attn_Wr, L0_attn_Wo, L0_attn_ln_g, L0_attn_ln_b)
    x = x + 0.5 * _L0_ffn_ref(_layernorm(x, axis=-1), L0_ffn_gate_weight, L0_ffn_w_gate, L0_ffn_w_up, L0_ffn_w_down, L0_ffn_ws_gate, L0_ffn_ws_up, L0_ffn_ws_down)
    return x

_drawn_inputs = setup_inputs


def setup_inputs(seed=0):
    import zlib

    import numpy as np

    out = dict(_drawn_inputs(seed))
    spreads = {'L0_attn_ln_g': (1.0, 0.2), 'L0_attn_ln_b': (0.0, 0.1)}
    factors = {'L0_ffn_gate_weight': 3.372,
     'L0_ffn_w_gate': 2.924,
     'L0_ffn_w_up': 2.887,
     'L0_ffn_w_down': 2.89,
     'L0_ffn_ws_gate': 3.501,
     'L0_ffn_ws_up': 3.46,
     'L0_ffn_ws_down': 3.463}
    for name, (base, spread) in spreads.items():
        noise = np.random.default_rng([zlib.crc32(name.encode()), seed]).standard_normal(out[name].shape)
        drawn = base * np.exp(spread * noise) if base else spread * noise
        out[name] = jnp.asarray(drawn.astype(out[name].dtype))
    for name, factor in factors.items():
        out[name] = (out[name] * factor).astype(out[name].dtype)
    return out
```

```python
from contextlib import ExitStack

import concourse.bass as bass
from concourse import mybir

F32 = mybir.dt.float32
F16 = mybir.dt.float16
U32 = mybir.dt.uint32
ALU = mybir.AluOpType
ACT = mybir.ActivationFunctionType

P = 128
EPS = 1e-5
TOPK = 2
ROUTE_SCALE = 2.5
W_SCALE = 256.0
W_UNSCALE = 1.0 / W_SCALE
STEPS = 20
HALF = STEPS // 2


def upto(s, per=1, part=0):
    i, off = s
    return i * per + (off * per + part + 1)


def residuals(phase, s, n_seq):
    i, off = s
    if phase == "A":
        return 2 if isinstance(i, int) and i + off == 0 else i * 4 + off * 4
    return min(4 * (i + off) + 6, 4 * n_seq) if isinstance(i, int) else i * 4 + (off * 4 + 6)


def step_tables(n_chunks, n_shared):
    pe_pre = {0: [("router_turn", 0, "A")], 11: [("router_turn", -1, "B")]}
    pe_mid = {2: [("scan_turn", -1)], 4: [("turn", -1, "o2")], 5: [("out_proj", -1)],
              7: [("turn", -1, "3")], 8: [("router", -1, "B")], 13: [("turn", 0, "2")],
              16: [("turn", 1, "1")], 18: [("router", 1, "A")], 0: [("r_proj", -1)]}
    pe_post = {17: [("kv_proj", 0, 0)], 18: [("kv_proj", 0, 1)]}

    act_pre = {0: [("router_turned", 0, "A")],
               11: [("router_turned", -1, "B")],
               18: [("k_copy", 0, 0)], 19: [("k_copy", 0, 1)]}
    act_post = {0: [("r_copy", -1, 0), ("r_copy", -1, 1)],
                2: [("o_copy", -1, 0), ("o_copy", -1, 1)],
                4: [("o_affine", -1, 0), ("o_affine", -1, 1), ("o_hi", -1, 0), ("o_hi", -1, 1)],
                7: [("x_hi", -1, "3", 0), ("x_hi", -1, "3", 1)],
                13: [("mix_in", 0, 0), ("mix_in", 0, 1)],
                15: [("mix_hi", 0, 0), ("mix_hi", 0, 1)],
                16: [("x_hi", 1, "1", 0), ("x_hi", 1, "1", 1), ("mix_hi", 0, 2), ("mix_hi", 0, 3)],
                18: [("mix_hi", 0, 4), ("mix_hi", 0, 5)]}

    dve_pre = {0: [("scan", -1, 1)], 1: [("receptance", -1)],
               3: [("stats", -1, "o")], 5: [("o_lo", -1, 0), ("o_lo", -1, 1)],
               6: [("stats", -1, "3")], 8: [("x_lo", -1, "3", 0), ("x_lo", -1, "3", 1)],
               10: [("combine", -1, "B")],
               12: [("stats", 0, "2")], 13: [("norm", 0, "2")], 14: [("shift_diff", 0)],
               15: [("mix", 0, 0), ("mix", 0, 1)], 16: [("mix", 0, 2), ("mix", 0, 3)],
               17: [("x_lo", 1, "1", 0), ("x_lo", 1, "1", 1), ("mix_lo", 0, 2), ("mix_lo", 0, 3)],
               18: [("kv", 0, 0), ("mix", 0, 4), ("mix", 0, 5)],
               19: [("kv", 0, 1), ("mix_lo", 0, 4), ("mix_lo", 0, 5)]}
    dve_post = {0: [("bonus", -1, 0), ("bonus", -1, 1)], 1: [("residual", -2, "B")],
                3: [("norm", -1, "o")], 5: [("out_residual", -1)], 6: [("norm", -1, "3")],
                8: [("top2", -1, "B")], 11: [("residual", 0, "A")],
                14: [("stats", 1, "1")], 15: [("norm", 1, "1")],
                16: [("mix_lo", 0, 0), ("mix_lo", 0, 1)],
                18: [("top2", 1, "A")], 19: [("combine", 1, "A"), ("scan", 0, 0)]}
    tables = {e: [] for e in ("pe", "act", "dve", "pool", "sp")}
    for k in range(STEPS):
        f, c = ("A", k) if k < HALF else ("B", k - HALF)
        seq = 0 if f == "A" else -1
        back = {n: (("A", k - n, 0) if k - n < HALF else ("B", k - n - HALF, -1)) if k >= n
                else ("B", HALF + k - n, -2) for n in (1, 2)}
        pe = pe_pre.get(k, []) + [("gate_up", seq, f, c)]
        if c >= n_shared:
            pe.append(("spread", seq, f, c))
        pe += pe_mid.get(k, []) + [("down", back[2][2], back[2][0], back[2][1])] + pe_post.get(k, [])
        tables["pe"].append(pe)
        last = (back[1][2], back[1][0], back[1][1])
        tables["act"].append([("hidden_hi", *last)] + act_pre.get(k, []) + [("silu", seq, f, c)]
                             + act_post.get(k, []))
        weigh = [("weigh", seq, f, c)] if c >= n_shared else []
        tables["dve"].append([("hidden_lo", *last)] + dve_pre.get(k, []) + [("gated", seq, f, c)]
                             + weigh + dve_post.get(k, []))
        tables["pool"].append({3: [("rstd", -1, "o")], 6: [("rstd", -1, "3")],
                               8: [("route_weights", -1, "B")], 12: [("rstd", 0, "2")],
                               14: [("rstd", 1, "1")], 18: [("route_weights", 1, "A")]}.get(k, []))
        tables["sp"].append({1: [("store", -2)], 11: [("load", 1)]}.get(k, []))
    return tables


def program(nc, x, w_chunks, w_attn, w_router, channels, out):
    NSEQ, T, C = x.shape
    NCH = w_chunks.shape[0]
    KC = C // P
    NT = T // P
    NE = w_router.shape[2]
    NSH = NCH - NE
    GU = 2 * KC * P
    assert NCH == HALF and T == 512 and C == 256
    MIX_K, MIX_V, MIX_R, DECAY, FIRST, LN_G, LN_B = range(7)

    WAHEAD = 3
    PHASE = {"1": "A", "3": "B"}
    tables = step_tables(NCH, NSH)
    FIRST_I, LOOP_I, END_I = -1, NSEQ - 1, NSEQ + 2
    prologue = [(i, k) for i in range(FIRST_I, 2) for k in range(STEPS) if (i, k) < (1, 2)]
    epilogue = [(i, k) for i in range(LOOP_I, END_I) for k in range(STEPS) if (i, k) >= (LOOP_I, 2)]

    def live(i, off):
        return not isinstance(i, int) or 0 <= i + off < NSEQ

    def walk(eng, table, do):
        def steps(i, k):
            for what, off, *args in table[k]:
                if live(i, off):
                    do[what]((i, off), *args)
        for i, k in prologue:
            steps(i, k)
        with eng.Fori(1, LOOP_I) as i:
            for k in range(2, STEPS):
                steps(i, k)
            for k in (0, 1):
                for what, off, *args in table[k]:
                    do[what]((i, off + 1), *args)
        for i, k in epilogue:
            steps(i, k)

    OUT_BANK, RING, SPREAD = 0, (2, 3, 4, 5), (6, 7)
    USES = {"gate_up": 2, "turn": 2, "scan_turn": 2, "out_proj": 2, "kv_proj": 2, "r_proj": 2,
            "router": 1}
    SPREADS = ("spread", "router_turn")
    banks = {}
    n_ring = n_spread = 0
    for k in [*range(2, STEPS), 0, 1]:
        for what, off, *args in tables["pe"][k]:
            for b in range(USES.get(what, 0)):
                banks[what, *args, b] = RING[n_ring % 4]
                n_ring += 1
            if what in SPREADS:
                banks[what, *args, 0] = SPREAD[n_spread % 2]
                n_spread += 1
    assert n_ring % 4 == 0 and n_spread % 2 == 0

    before, held = {}, {}
    for i in range(FIRST_I, END_I):
        for k in range(STEPS):
            for what, off, *args in tables["pe"][k]:
                if live(i, off):
                    for b in range(USES.get(what, 0) or (what in SPREADS)):
                        bank = banks[what, *args, b]
                        if bank in held:
                            t, s = held[bank]
                            before[what, *args, b, i + off] = (t, s - i - off)
                        held[bank] = ((what, *args, b), i + off)

    with ExitStack() as ctx:
        def sb(name, shape, dt=F32):
            return ctx.enter_context(nc.sbuf_tensor(name, shape, dt))

        def sem(name):
            return ctx.enter_context(nc.semaphore(name))

        ps = ctx.enter_context(nc.psum_tensor("ps", [P, 8, 512], F32))

        w_hi = sb("w_hi", [P, NCH, GU + C], F16)
        w_lo = sb("w_lo", [P, NCH, GU + C], F16)
        a_hi = sb("a_hi", [P, 4, KC, C], F16)
        a_lo = sb("a_lo", [P, 4, KC, C], F16)
        r_hi = sb("r_hi", [P, KC, NE], F16)
        r_lo = sb("r_lo", [P, KC, NE], F16)
        r_stage = sb("r_stage", [P, KC, NE])
        chan = sb("chan", [P, 7, KC])
        decay = sb("decay", [P, KC])
        arena = sb("arena", [P, NCH * (GU + C) + 4 * KC * C])
        w_stage = arena[:, 0:NCH * (GU + C)].rearrange("p (c n) -> p c n", c=NCH)
        a_stage = arena[:, NCH * (GU + C):].rearrange("p (a k n) -> p a k n", a=4, k=KC)
        mix32 = arena[:, 0:6 * T].rearrange("p (j t) -> p j t", j=6)

        def tile_at(n):
            return arena[:, (6 + 2 * n) * T:(8 + 2 * n) * T].rearrange("p (m t) -> p m t", m=KC)

        diff, k_sb, kv_sb, state, r_sb, o_aff = (tile_at(n) for n in range(6))

        ident = sb("ident", [P, P])
        ident16 = sb("ident16", [P, P], F16)
        select = sb("select", [2 * NE, NE, P], F16)
        experts = sb("experts", [P, NT, TOPK, NE])
        neg_half = sb("neg_half", [P, NT])
        neg_one = sb("neg_one", [P, NT, TOPK])
        inv_e = sb("inv_e", [P, NT, TOPK])
        euler = sb("euler", [P, KC])
        eps_t = sb("eps_t", [P, NT])
        tiny = sb("tiny", [P, NT])
        ones = sb("ones", [P, NT, TOPK])
        route_scale = sb("route_scale", [P, NT, TOPK])

        x0 = sb("x0", [P, NT, C])
        x1 = sb("x1", [P, NT, C])
        x2 = sb("x2", [P, NT, C])
        x3 = sb("x3", [P, NT, C])
        o_tok = sb("o_tok", [P, NT, C])
        LNS = ("1", "2", "o", "3")
        normed = {n: sb(f"normed{n}", [P, NT, C]) for n in ("1", "2", "3")} | {"o": o_tok}
        ln_in = {"1": x0, "2": x1, "o": o_tok, "3": x2}
        stat = {n: sb(f"stat{n}", [P, NT, 6]) for n in LNS}
        mean_var = {n: sb(f"mean_var{n}", [P, NT, 2]) for n in LNS}
        var_eps = {n: sb(f"var_eps{n}", [P, NT]) for n in LNS}
        rstd_t = {n: sb(f"rstd{n}", [P, NT]) for n in LNS}

        xh = {f: sb(f"xh{f}", [P, KC, T], F16) for f in "AB"}
        xl = {f: sb(f"xl{f}", [P, KC, T], F16) for f in "AB"}
        shifted = sb("shifted", [P, KC, T + 1])
        mix_h = sb("mix_h", [P, 6, T], F16)
        mix_l = sb("mix_l", [P, 6, T], F16)
        oh = sb("oh", [P, KC, T], F16)
        ol = sb("ol", [P, KC, T], F16)

        silu_t = sb("silu_t", [P, 2, T])
        gated_t = sb("gated_t", [P, 2, T])
        hid = sb("hid", [P, 2, T])
        hid_h = sb("hid_h", [P, 4, T], F16)
        hid_l = sb("hid_l", [P, 4, T], F16)

        logits = {f: sb(f"logits{f}", [P, NT, NE]) for f in "AB"}
        best = {f: sb(f"best{f}", [P, NT, NE]) for f in "AB"}
        best_at = {f: sb(f"best_at{f}", [P, NT, NE], U32) for f in "AB"}
        p_exp = sb("p_exp", [P, NT, TOPK])
        p_one = sb("p_one", [P, NT, TOPK])
        score = sb("score", [P, NT, TOPK])
        score_sum = sb("score_sum", [P, NT])
        score_eps = sb("score_eps", [P, NT])
        score_inv = sb("score_inv", [P, NT])
        share = sb("share", [P, NT, TOPK])
        share_s = {f: sb(f"share_s{f}", [P, NT, TOPK]) for f in "AB"}
        chosen = sb("chosen", [P, NT, TOPK, NE])
        chosen_w = sb("chosen_w", [P, NT, TOPK, NE])
        comb = sb("comb", [P, NT, NE])
        comb16 = sb("comb16", [P, NT, 2 * NE], F16)
        comb_t = {f: sb(f"comb_t{f}", [2 * NE, T], F16) for f in "AB"}

        w_in = [sem(f"w_in{c}") for c in range(NCH)]
        attn_in, router_in, chan_in = sem("attn_in"), sem("router_in"), sem("chan_in")
        x_in, stored = sem("x_in"), sem("stored")
        w_hi_done, w_split = sem("w_hi_done"), sem("w_split")
        const_set, consts = sem("const_set"), sem("consts")
        gate_done = {f: sem(f"gate_done{f}") for f in "AB"}
        up_done = {f: sem(f"up_done{f}") for f in "AB"}
        down_done = {f: sem(f"down_done{f}") for f in "AB"}
        spread_done = {f: sem(f"spread_done{f}") for f in "AB"}
        silu_done = {f: sem(f"silu_done{f}") for f in "AB"}
        gated_done = {f: sem(f"gated_done{f}") for f in "AB"}
        weigh_done = {f: sem(f"weigh_done{f}") for f in "AB"}
        hi_done = {f: sem(f"hi_done{f}") for f in "AB"}
        lo_done = {f: sem(f"lo_done{f}") for f in "AB"}
        residual_done, x2_done = sem("residual_done"), sem("x2_done")
        stats_done = {n: sem(f"stats_done{n}") for n in LNS}
        moments_done = {n: sem(f"moments_done{n}") for n in LNS}
        var_done = {n: sem(f"var_done{n}") for n in LNS}
        rstd_done = {n: sem(f"rstd_done{n}") for n in LNS}
        norm_done = {n: sem(f"norm_done{n}") for n in LNS}
        turned = {n: sem(f"turned{n}") for n in ("1", "2", "o2", "3")}
        turned_hi = {n: sem(f"turned_hi{n}") for n in ("1", "3")}
        turned_lo = {n: sem(f"turned_lo{n}") for n in ("1", "3")}
        mix_in_done, diff_done = sem("mix_in_done"), sem("diff_done")
        mix_done, mix_hi_done, mix_lo_done = sem("mix_done"), sem("mix_hi_done"), sem("mix_lo_done")
        k_done, v_done, r_done = sem("k_done"), sem("v_done"), sem("r_done")
        k_copied, r_copied = sem("k_copied"), sem("r_copied")
        kv_done, scan_done, bonus_done = sem("kv_done"), sem("scan_done"), sem("bonus_done")
        mixed_done, scan_turned, o_copied = sem("mixed_done"), sem("scan_turned"), sem("o_copied")
        o_affine_done, o_hi_done, o_lo_done = sem("o_affine_done"), sem("o_hi_done"), sem("o_lo_done")
        out_proj_done = sem("out_proj_done")
        router_done = {f: sem(f"router_done{f}") for f in "AB"}
        logits_out = {f: sem(f"logits_out{f}") for f in "AB"}
        max_done = {f: sem(f"max_done{f}") for f in "AB"}
        top2_done = {f: sem(f"top2_done{f}") for f in "AB"}
        pool_route = {f: sem(f"pool_route{f}") for f in "AB"}
        shares_done = {f: sem(f"shares_done{f}") for f in "AB"}
        comb_step = {f: sem(f"comb_step{f}") for f in "AB"}
        comb_done = {f: sem(f"comb_done{f}") for f in "AB"}
        comb_turned = {f: sem(f"comb_turned{f}") for f in "AB"}
        comb_copied = {f: sem(f"comb_copied{f}") for f in "AB"}

        def own_wait(eng, signal, value):
            eng.wait_ge(consts, 4)
            eng.wait_ge(signal, value)

        def silu_before(s, f, c):
            i, off = s
            if c >= 2:
                return s, f, c - 2
            prev, other = ((i, off - 2), "B") if f == "A" else ((i, off + 1), "A")
            if live(i, prev[1]):
                return prev, other, c + NCH - 2
            return ((i, off - 1), f, c + NCH - 2) if live(i, off - 1) else (None, f, c)

        def released(task, s):
            what, *args, b = task
            if what == "gate_up":
                f, c = args
                return (silu_done, gated_done)[b][f], upto(s, NCH, c)
            if what == "turn":
                n = args[0]
                if n == "2":
                    return mix_in_done, upto(s, KC, b)
                if n == "o2":
                    return o_affine_done, upto(s, KC, b)
                return turned_lo[n], upto(s, KC, b)
            if what == "scan_turn":
                return o_copied, upto(s, 2, b)
            if what == "out_proj":
                return x2_done, upto(s, 2, b)
            if what == "kv_proj":
                return (k_copied, kv_done)[b], upto(s, KC, args[0])
            if what == "r_proj":
                return r_copied, upto(s, KC, b)
            if what == "router":
                return logits_out[args[0]], upto(s)
            if what == "spread":
                f, c = args
                return weigh_done[f], upto(s, NE, c - NSH)
            return comb_copied[args[0]], upto(s)

        block = ctx.enter_context(nc.Block())

        @block.sync
        def _(sp):
            x_tok = x.rearrange("s (j p) c -> s p j c", p=P)
            out_tok = out.rearrange("s (j p) c -> s p j c", p=P)

            def load_next(s):
                i, off = s
                if isinstance(i, int) and i + off == 0:
                    return
                sp.wait_ge(residual_done, residuals("A", (i, off - 1), NSEQ))
                sp.dma_start(x0[:], x_tok[i + off]).then_inc(x_in, 16)

            def store(s):
                i, off = s
                sp.wait_ge(residual_done, residuals("B", s, NSEQ))
                sp.dma_start(out_tok[i + off], x3[:]).then_inc(stored, 16)

            sp.dma_start(x0[:], x_tok[0]).then_inc(x_in, 16)
            sp.dma_start(r_stage[:], w_router).then_inc(router_in, 16)
            for c in range(0, NCH):
                sp.dma_start(w_stage[:, c, :], w_chunks[c]).then_inc(w_in[c], 16)
            sp.dma_start(a_stage, w_attn).then_inc(attn_in, 16)
            walk(sp, tables["sp"], {"load": load_next, "store": store})
            sp.wait_ge(stored, 16 * NSEQ)

        @block.gpsimd
        def _(pool):
            g = nc.gpsimd
            g.memset(ident[:], 0.0).then_inc(const_set, 1)
            g.memset(ident16[:], 0.0).then_inc(const_set, 1)
            g.memset(select[:], 0.0).then_inc(const_set, 1)
            g.memset(neg_half[:], -0.5).then_inc(const_set, 1)
            g.memset(neg_one[:], -1.0).then_inc(const_set, 1)
            g.memset(inv_e[:], 0.36787944117144233).then_inc(const_set, 1)
            g.memset(euler[:], 2.718281828459045).then_inc(const_set, 1)
            g.memset(shifted[:, :, 0:1], 0.0).then_inc(const_set, 1)
            g.memset(eps_t[:], EPS).then_inc(const_set, 1)
            g.memset(tiny[:], 1e-20).then_inc(const_set, 1)
            g.memset(ones[:], 1.0).then_inc(const_set, 1)
            g.memset(route_scale[:], ROUTE_SCALE).then_inc(const_set, 1)
            pool.wait_ge(const_set, 12)
            for m in (ident, ident16):
                g.affine_select(out=m[:], in_=m[:], compare_op=ALU.not_equal, fill=1.0, base=0,
                                pattern=[[-1, P]], channel_multiplier=1).then_inc(consts, 1)
            g.affine_select(out=select[:], in_=select[:], compare_op=ALU.not_equal, fill=1.0, base=0,
                            pattern=[[-1, NE], [0, P]], channel_multiplier=1).then_inc(const_set, 1)
            pool.wait_ge(const_set, 13)
            g.affine_select(out=select[:], in_=select[:], compare_op=ALU.not_equal, fill=1.0,
                            base=-NE, pattern=[[-1, NE], [0, P]], channel_multiplier=1)\
                .then_inc(consts, 1)
            pool.wait_ge(chan_in, 16)
            g.tensor_tensor(decay[:], euler[:], chan[:, DECAY, :], ALU.pow).then_inc(consts, 1)

            def rstd(s, n):
                pool.wait_ge(moments_done[n], upto(s))
                g.tensor_tensor(var_eps[n][:], mean_var[n][:, :, 1], eps_t[:], ALU.add)\
                    .then_inc(var_done[n], 1)
                pool.wait_ge(var_done[n], upto(s))
                g.tensor_tensor(rstd_t[n][:], var_eps[n][:], neg_half[:], ALU.pow)\
                    .then_inc(rstd_done[n], 1)

            def route_weights(s, f):
                n = 7
                pool.wait_ge(top2_done[f], upto(s))
                g.tensor_tensor(p_exp[:], inv_e[:], best[f][:, :, 0:TOPK], ALU.pow)\
                    .then_inc(pool_route[f], 1)
                pool.wait_ge(pool_route[f], upto(s, n, 0))
                g.tensor_tensor(p_one[:], p_exp[:], ones[:], ALU.add)\
                    .then_inc(pool_route[f], 1)
                pool.wait_ge(pool_route[f], upto(s, n, 1))
                g.tensor_tensor(score[:], p_one[:], neg_one[:], ALU.pow).then_inc(pool_route[f], 1)
                pool.wait_ge(pool_route[f], upto(s, n, 2))
                g.tensor_tensor(score_sum[:], score[:, :, 0], score[:, :, 1], ALU.add)\
                    .then_inc(pool_route[f], 1)
                pool.wait_ge(pool_route[f], upto(s, n, 3))
                g.tensor_tensor(score_eps[:], score_sum[:], tiny[:], ALU.add)\
                    .then_inc(pool_route[f], 1)
                pool.wait_ge(pool_route[f], upto(s, n, 4))
                g.tensor_tensor(score_inv[:], score_eps[:], neg_one[:, :, 0], ALU.pow)\
                    .then_inc(pool_route[f], 1)
                pool.wait_ge(pool_route[f], upto(s, n, 5))
                g.tensor_tensor(share[:], score[:], score_inv[:].unsqueeze(2).to_broadcast([P, NT, TOPK]),
                                ALU.mult).then_inc(pool_route[f], 1)
                pool.wait_ge(pool_route[f], upto(s, n, 6))
                g.tensor_tensor(share_s[f][:], share[:], route_scale[:], ALU.mult)\
                    .then_inc(shares_done[f], 1)

            walk(pool, tables["pool"], {"rstd": rstd, "route_weights": route_weights})

        @block.tensor
        def _(pe):
            def bank_free(s, *task_b):
                i, off = s
                seq = i + off if isinstance(i, int) else 7
                if (*task_b, seq) in before:
                    t, rel = before[(*task_b, seq)]
                    pe.wait_ge(*released(t, (i, off + rel)))
                return banks[task_b]

            def three(out_ap, hi_w, lo_w, hi_x, lo_x, first, last, lone):
                nc.tensor.matmul(out_ap, hi_w, hi_x, start=first, stop=False, skip_group_check=lone)
                nc.tensor.matmul(out_ap, lo_w, hi_x, start=False, stop=False, skip_group_check=lone)
                return nc.tensor.matmul(out_ap, hi_w, lo_x, start=False, stop=last,
                                        skip_group_check=lone)

            def gate_up(s, f, c):
                i, off = s
                if c == 0:
                    pe.wait_ge(turned_lo["1" if f == "A" else "3"], upto(s, KC, KC - 1))
                if f == "A" and isinstance(i, int) and i + off == 0:
                    pe.wait_ge(w_split, c + 2)
                for b, done in ((0, gate_done), (1, up_done)):
                    bank = bank_free(s, "gate_up", f, c, b)
                    for k in range(KC):
                        cols = slice(k * 2 * P + b * P, k * 2 * P + (b + 1) * P)
                        mm = three(ps[:, bank, :], w_hi[:, c, cols], w_lo[:, c, cols],
                                   xh[f][:, k, :], xl[f][:, k, :], k == 0, k == KC - 1, False)
                    mm.then_inc(done[f], 1)

            def spread(s, f, c):
                if c == NSH:
                    pe.wait_ge(comb_copied[f], upto(s))
                bank = bank_free(s, "spread", f, c, 0)
                nc.tensor.matmul(ps[:, bank, :], select[:, c - NSH, :], comb_t[f][:], start=True,
                                 stop=True).then_inc(spread_done[f], 1)

            def down(s, f, c):
                i, off = s
                pe.wait_ge(lo_done[f], upto(s, NCH, c))
                if c == 0 and not (f == "A" and isinstance(i, int) and i + off == 0):
                    if f == "A":
                        pe.wait_ge(residual_done, i * 4 + (off * 4 - 2))
                    else:
                        v = i * 4 + (off * 4 + 4)
                        pe.wait_ge(residual_done, min(v, 4 * NSEQ - 2) if isinstance(i, int) else v)
                b = ((0 if f == "A" else NCH) + c) % 4
                for j in range(NT):
                    tok = slice(j * P, (j + 1) * P)
                    half = ps[:, OUT_BANK + j // 2, (j % 2) * C:(j % 2 + 1) * C]
                    wh, wl = w_hi[:, c, GU:], w_lo[:, c, GU:]
                    nc.tensor.matmul(half, hid_h[:, b, tok], wh, start=(c == 0 and j % 2 == 0),
                                     stop=False, skip_group_check=True)
                    nc.tensor.matmul(half, hid_h[:, b, tok], wl, start=False, stop=False,
                                     skip_group_check=True)
                    mm = nc.tensor.matmul(half, hid_l[:, b, tok], wh, start=False,
                                          stop=(c == NCH - 1 and j % 2 == 1), skip_group_check=True)
                mm.then_inc(down_done[f], 1)

            def turn(s, n):
                pe.wait_ge(norm_done[n[0]], upto(s))
                for m in range(KC):
                    bank = bank_free(s, "turn", n, m)
                    for j in range(NT):
                        mm = nc.tensor.transpose(ps[:, bank, j * P:(j + 1) * P],
                                                 normed[n[0]][:, j, m * P:(m + 1) * P], ident[:])
                    mm.then_inc(turned[n], 1)

            def kv_proj(s, m):
                if m == 0:
                    pe.wait_ge(mix_lo_done, upto(s, 6, 3))
                    first_attn(s)
                for b, done in ((0, k_done), (1, v_done)):
                    bank = bank_free(s, "kv_proj", m, b)
                    project(bank, b, m).then_inc(done, 1)

            def project(bank, which, m):
                for k in range(KC):
                    cols = slice(m * P, (m + 1) * P)
                    mm = three(ps[:, bank, :], a_hi[:, which, k, cols], a_lo[:, which, k, cols],
                               mix_h[:, which * KC + k, :], mix_l[:, which * KC + k, :],
                               k == 0, k == KC - 1, False)
                return mm

            def first_attn(s):
                if isinstance(s[0], int) and sum(s) == 0:
                    pe.wait_ge(w_split, NCH + 2)

            def r_proj(s):
                pe.wait_ge(mix_lo_done, upto(s, 6, 5))
                for m in range(KC):
                    bank = bank_free(s, "r_proj", m)
                    project(bank, 2, m).then_inc(r_done, 1)

            def scan_turn(s):
                pe.wait_ge(mixed_done, upto(s))
                for b in range(2):
                    bank = bank_free(s, "scan_turn", b)
                    for j in range(2):
                        for m in range(KC):
                            t0 = (2 * b + j) * P
                            mm = nc.tensor.transpose(ps[:, bank, j * C + m * P:j * C + (m + 1) * P],
                                                     state[:, m, t0:t0 + P], ident[:])
                    mm.then_inc(scan_turned, 1)

            def out_proj(s):
                pe.wait_ge(o_lo_done, upto(s, KC, KC - 1))
                for b in range(2):
                    bank = bank_free(s, "out_proj", b)
                    for j in range(2):
                        tok = slice((2 * b + j) * P, (2 * b + j + 1) * P)
                        half = ps[:, bank, j * C:(j + 1) * C]
                        for k in range(KC):
                            nc.tensor.matmul(half, oh[:, k, tok], a_hi[:, 3, k, :],
                                             start=(k == 0 and j == 0), stop=False,
                                             skip_group_check=True)
                            nc.tensor.matmul(half, oh[:, k, tok], a_lo[:, 3, k, :], start=False,
                                             stop=False, skip_group_check=True)
                            mm = nc.tensor.matmul(half, ol[:, k, tok], a_hi[:, 3, k, :], start=False,
                                                  stop=(k == KC - 1 and j == 1),
                                                  skip_group_check=True)
                    mm.then_inc(out_proj_done, 1)

            def router(s, f):
                pe.wait_ge(turned_lo["1" if f == "A" else "3"], upto(s, KC, KC - 1))
                if f == "A" and isinstance(s[0], int) and sum(s) == 0:
                    pe.wait_ge(w_split, 1)
                bank = bank_free(s, "router", f, 0)
                for j in range(NT):
                    tok = slice(j * P, (j + 1) * P)
                    cell = ps[:, bank, j * NE:(j + 1) * NE]
                    for k in range(KC):
                        nc.tensor.matmul(cell, xh[f][:, k, tok], r_hi[:, k, :],
                                         start=(j == 0 and k == 0), stop=False, skip_group_check=True)
                        nc.tensor.matmul(cell, xh[f][:, k, tok], r_lo[:, k, :], start=False,
                                         stop=False, skip_group_check=True)
                        mm = nc.tensor.matmul(cell, xl[f][:, k, tok], r_hi[:, k, :], start=False,
                                              stop=(j == NT - 1 and k == KC - 1),
                                              skip_group_check=True)
                mm.then_inc(router_done[f], 1)

            def router_turn(s, f):
                pe.wait_ge(comb_done[f], upto(s))
                bank = bank_free(s, "router_turn", f, 0)
                cells = ps[0:2 * NE, bank, :].bitcast(F16)
                for j in range(NT):
                    mm = nc.tensor.transpose(cells[:, j * P:(j + 1) * P], comb16[:, j, :], ident16[:])
                mm.then_inc(comb_turned[f], 1)

            pe.wait_ge(consts, 3)
            walk(pe, tables["pe"], {
                "gate_up": gate_up, "spread": spread, "down": down, "turn": turn,
                "kv_proj": kv_proj, "r_proj": r_proj, "scan_turn": scan_turn, "out_proj": out_proj,
                "router": router, "router_turn": router_turn})

        @block.scalar
        def _(act):
            act.dma_start(chan[:], channels).then_inc(chan_in, 16)

            def split_weights(c):
                if c < 0:
                    act.wait_ge(router_in, 16)
                    nc.scalar.activation(r_hi[:], r_stage[:], ACT.Copy, scale=W_SCALE)\
                        .then_inc(w_hi_done, 1)
                elif c < NCH:
                    act.wait_ge(w_in[c], 16)
                    nc.scalar.activation(w_hi[:, c, :], w_stage[:, c, :], ACT.Copy, scale=W_SCALE)\
                        .then_inc(w_hi_done, 1)
                else:
                    act.wait_ge(attn_in, 16)
                    nc.scalar.activation(a_hi[:], a_stage, ACT.Copy, scale=W_SCALE)\
                        .then_inc(w_hi_done, 1)

            def silu(s, f, c):
                if f == "A" and isinstance(s[0], int) and sum(s) == 0:
                    if c + WAHEAD <= NCH:
                        split_weights(c + WAHEAD)
                act.wait_ge(gate_done[f], upto(s, NCH, c))
                last, lf, lc = silu_before(s, f, c)
                if last is not None:
                    act.wait_ge(gated_done[lf], upto(last, NCH, lc))
                nc.scalar.activation(silu_t[:, c % 2, :], ps[:, banks["gate_up", f, c, 0], :],
                                     ACT.Silu, scale=W_UNSCALE).then_inc(silu_done[f], 1)

            def hidden_hi(s, f, c):
                if c < NSH:
                    act.wait_ge(gated_done[f], upto(s, NCH, c))
                else:
                    act.wait_ge(weigh_done[f], upto(s, NE, c - NSH))
                b = ((0 if f == "A" else NCH) + c) % 4
                nc.scalar.copy(hid_h[:, b, :], hid[:, c % 2, :]).then_inc(hi_done[f], 1)

            def x_hi(s, n, m):
                act.wait_ge(turned[n], upto(s, KC, m))
                nc.scalar.copy(xh[PHASE[n]][:, m, :], ps[:, banks["turn", n, m], :])\
                    .then_inc(turned_hi[n], 1)

            def mix_in(s, m):
                act.wait_ge(turned["2"], upto(s, KC, m))
                nc.scalar.copy(shifted[:, m, 1:T + 1], ps[:, banks["turn", "2", m], :])\
                    .then_inc(mix_in_done, 1)

            def mix_hi(s, j):
                act.wait_ge(mix_done, upto(s, 6, j))
                nc.scalar.copy(mix_h[:, j, :], mix32[:, j, :]).then_inc(mix_hi_done, 1)

            def k_copy(s, m):
                act.wait_ge(k_done, upto(s, KC, m))
                nc.scalar.activation(k_sb[:, m, :], ps[:, banks["kv_proj", m, 0], :], ACT.Copy,
                                     scale=W_UNSCALE).then_inc(k_copied, 1)

            def r_copy(s, m):
                act.wait_ge(r_done, upto(s, KC, m))
                nc.scalar.activation(r_sb[:, m, :], ps[:, banks["r_proj", m], :], ACT.Copy,
                                     scale=W_UNSCALE).then_inc(r_copied, 1)

            def o_copy(s, b):
                act.wait_ge(scan_turned, upto(s, 2, b))
                nc.scalar.copy(o_tok[:, 2 * b:2 * b + 2, :],
                               ps[:, banks["scan_turn", b], :].rearrange("p (j c) -> p j c", j=2))\
                    .then_inc(o_copied, 1)

            def o_affine(s, m):
                act.wait_ge(turned["o2"], upto(s, KC, m))
                nc.scalar.activation(o_aff[:, m, :], ps[:, banks["turn", "o2", m], :], ACT.Identity,
                                     bias=chan[:, LN_B, m:m + 1], scale=chan[:, LN_G, m:m + 1])\
                    .then_inc(o_affine_done, 1)

            def o_hi(s, m):
                act.wait_ge(o_affine_done, upto(s, KC, m))
                nc.scalar.copy(oh[:, m, :], o_aff[:, m, :]).then_inc(o_hi_done, 1)

            def router_turned(s, f):
                act.wait_ge(comb_turned[f], upto(s))
                cells = ps[0:2 * NE, banks["router_turn", f, 0], :].bitcast(F16)
                nc.scalar.copy(comb_t[f][:], cells[:, 0:T]).then_inc(comb_copied[f], 1)

            act.wait_ge(consts, 1)
            nc.scalar.activation(silu_t[:, 1, 0:1], ident[:, 0:1], ACT.Silu)
            for c in range(-1, WAHEAD):
                split_weights(c)
            act.wait_ge(chan_in, 16)
            walk(act, tables["act"], {
                "silu": silu, "hidden_hi": hidden_hi, "x_hi": x_hi, "mix_in": mix_in,
                "mix_hi": mix_hi, "k_copy": k_copy, "r_copy": r_copy, "o_copy": o_copy,
                "o_affine": o_affine, "o_hi": o_hi, "router_turned": router_turned})

        @block.vector
        def _(dve):
            v = nc.vector

            def split_weights(c):
                dve.wait_ge(w_hi_done, c + 2)
                if c < 0:
                    hi, lo, full = r_hi[:], r_lo[:], r_stage[:]
                elif c < NCH:
                    hi, lo, full = w_hi[:, c, :], w_lo[:, c, :], w_stage[:, c, :]
                else:
                    flat = "p a k n -> p (a k n)"
                    hi, lo, full = (a_hi[:].rearrange(flat), a_lo[:].rearrange(flat),
                                    a_stage.rearrange(flat))
                v.scalar_tensor_tensor(out=lo, in0=full, scalar=W_SCALE, in1=hi, op0=ALU.mult,
                                       op1=ALU.subtract).then_inc(w_split, 1)

            def gated(s, f, c):
                if f == "A" and isinstance(s[0], int) and sum(s) == 0:
                    if c + WAHEAD <= NCH:
                        split_weights(c + WAHEAD)
                dve.wait_ge(silu_done[f], upto(s, NCH, c))
                dve.wait_ge(up_done[f], upto(s, NCH, c))
                to = hid if c < NSH else gated_t
                v.scalar_tensor_tensor(out=to[:, c % 2, :], in0=ps[:, banks["gate_up", f, c, 1], :],
                                       scalar=W_UNSCALE, in1=silu_t[:, c % 2, :], op0=ALU.mult,
                                       op1=ALU.mult).then_inc(gated_done[f], 1)

            def weigh(s, f, c):
                dve.wait_ge(gated_done[f], upto(s, NCH, c))
                dve.wait_ge(spread_done[f], upto(s, NE, c - NSH))
                v.tensor_tensor(hid[:, c % 2, :], gated_t[:, c % 2, :],
                                ps[:, banks["spread", f, c, 0], :], ALU.mult)\
                    .then_inc(weigh_done[f], 1)

            def hidden_lo(s, f, c):
                dve.wait_ge(hi_done[f], upto(s, NCH, c))
                b = ((0 if f == "A" else NCH) + c) % 4
                v.tensor_tensor(hid_l[:, b, :], hid[:, c % 2, :], hid_h[:, b, :], ALU.subtract)\
                    .then_inc(lo_done[f], 1)

            def residual(s, f):
                i, off = s
                dve.wait_ge(down_done[f], upto(s, NCH, NCH - 1))
                if f == "B":
                    dve.wait_ge(x2_done, upto(s, 2, 1))
                    if not (isinstance(i, int) and i + off == 0):
                        dve.wait_ge(stored, i * 16 + off * 16)
                src, dst = (x0, x1) if f == "A" else (x2, x3)
                for b in range(2):
                    v.scalar_tensor_tensor(
                        out=dst[:, 2 * b:2 * b + 2, :].rearrange("p j c -> p (j c)"),
                        in0=ps[:, OUT_BANK + b, :], scalar=0.5 * W_UNSCALE,
                        in1=src[:, 2 * b:2 * b + 2, :].rearrange("p j c -> p (j c)"),
                        op0=ALU.mult, op1=ALU.add).then_inc(residual_done, 1)

            def stats(s, n):
                of_all = upto(s) if isinstance(s[0], int) else dve.to_reg(upto(s))
                if n == "1":
                    dve.wait_ge(x_in, upto(s, 16, 15))
                elif n == "2":
                    dve.wait_ge(residual_done, residuals("A", s, NSEQ))
                elif n == "o":
                    dve.wait_ge(o_copied, upto(s, 2, 1))
                else:
                    dve.wait_ge(x2_done, upto(s, 2, 1))
                for j in range(NT):
                    ins = v.bn_stats(out=stat[n][:, j, :], in_=ln_in[n][:, j, :])
                ins.then_inc(stats_done[n], 1)
                own_wait(dve, stats_done[n], of_all)
                for j in range(NT):
                    ins = v.bn_aggr(out=mean_var[n][:, j, :], in_=stat[n][:, j, :])
                ins.then_inc(moments_done[n], 1)

            def norm(s, n):
                dve.wait_ge(moments_done[n], upto(s))
                dve.wait_ge(rstd_done[n], upto(s))
                for j in range(NT):
                    ins = v.tensor_scalar(normed[n][:, j, :], ln_in[n][:, j, :],
                                          mean_var[n][:, j, 0:1], rstd_t[n][:, j:j + 1],
                                          ALU.subtract, ALU.mult)
                ins.then_inc(norm_done[n], 1)

            def x_lo(s, n, m):
                dve.wait_ge(turned_hi[n], upto(s, KC, m))
                v.tensor_tensor(xl[PHASE[n]][:, m, :], ps[:, banks["turn", n, m], :],
                                xh[PHASE[n]][:, m, :], ALU.subtract).then_inc(turned_lo[n], 1)

            def shift_diff(s):
                dve.wait_ge(mix_in_done, upto(s, KC, KC - 1))
                v.tensor_tensor(diff, shifted[:, :, 1:T + 1], shifted[:, :, 0:T], ALU.subtract)\
                    .then_inc(diff_done, 1)

            def mix(s, j):
                which, m = divmod(j, KC)
                dve.wait_ge(diff_done, upto(s))
                v.scalar_tensor_tensor(out=mix32[:, j, :], in0=diff[:, m, :],
                                       scalar=chan[:, MIX_K + which, m:m + 1],
                                       in1=shifted[:, m, 0:T], op0=ALU.mult, op1=ALU.add)\
                    .then_inc(mix_done, 1)

            def mix_lo(s, j):
                dve.wait_ge(mix_hi_done, upto(s, 6, j))
                v.tensor_tensor(mix_l[:, j, :], mix32[:, j, :], mix_h[:, j, :], ALU.subtract)\
                    .then_inc(mix_lo_done, 1)

            def kv(s, m):
                dve.wait_ge(k_copied, upto(s, KC, m))
                dve.wait_ge(v_done, upto(s, KC, m))
                v.scalar_tensor_tensor(out=kv_sb[:, m, :], in0=ps[:, banks["kv_proj", m, 1], :],
                                       scalar=W_UNSCALE, in1=k_sb[:, m, :], op0=ALU.mult,
                                       op1=ALU.mult).then_inc(kv_done, 1)

            def scan(s, m):
                dve.wait_ge(kv_done, upto(s, KC, m))
                v.tensor_tensor_scan(state[:, m, :], decay[:, m:m + 1].to_broadcast([P, T]),
                                     kv_sb[:, m, :], 0.0, ALU.mult, ALU.add).then_inc(scan_done, 1)

            def bonus(s, m):
                dve.wait_ge(scan_done, upto(s, KC, m))
                v.scalar_tensor_tensor(out=state[:, m, :], in0=kv_sb[:, m, :],
                                       scalar=chan[:, FIRST, m:m + 1], in1=state[:, m, :],
                                       op0=ALU.mult, op1=ALU.add).then_inc(bonus_done, 1)

            def receptance(s):
                dve.wait_ge(bonus_done, upto(s, KC, KC - 1))
                dve.wait_ge(r_copied, upto(s, KC, KC - 1))
                v.tensor_tensor(state, state, r_sb, ALU.mult).then_inc(mixed_done, 1)

            def o_lo(s, m):
                dve.wait_ge(o_hi_done, upto(s, KC, m))
                v.tensor_tensor(ol[:, m, :], o_aff[:, m, :], oh[:, m, :], ALU.subtract)\
                    .then_inc(o_lo_done, 1)

            def out_residual(s):
                for b in range(2):
                    dve.wait_ge(out_proj_done, upto(s, 2, b))
                    v.scalar_tensor_tensor(
                        out=x2[:, 2 * b:2 * b + 2, :].rearrange("p j c -> p (j c)"),
                        in0=ps[:, banks["out_proj", b], :], scalar=W_UNSCALE,
                        in1=x1[:, 2 * b:2 * b + 2, :].rearrange("p j c -> p (j c)"),
                        op0=ALU.mult, op1=ALU.add).then_inc(x2_done, 1)

            def top2(s, f):
                dve.wait_ge(router_done[f], upto(s))
                v.tensor_scalar(logits[f][:].rearrange("p j e -> p (j e)"),
                                ps[:, banks["router", f, 0], 0:NT * NE], W_UNSCALE, None, ALU.mult)\
                    .then_inc(logits_out[f], 1)
                own_wait(dve, logits_out[f], upto(s))
                for j in range(NT):
                    ins = v.max(out=best[f][:, j, :], in_=logits[f][:, j, :])
                ins.then_inc(max_done[f], 1)
                own_wait(dve, max_done[f], upto(s))
                for j in range(NT):
                    ins = v.max_index(out=best_at[f][:, j, :], in_max=best[f][:, j, :],
                                      in_values=logits[f][:, j, :])
                ins.then_inc(top2_done[f], 1)

            def combine(s, f):
                all_ = [P, NT, TOPK, NE]
                dve.wait_ge(top2_done[f], upto(s))
                v.tensor_tensor(chosen[:], experts[:],
                                best_at[f][:, :, 0:TOPK].unsqueeze(3).to_broadcast(all_),
                                ALU.is_equal).then_inc(comb_step[f], 1)
                dve.wait_ge(comb_step[f], upto(s, 4, 0))
                dve.wait_ge(shares_done[f], upto(s))
                v.tensor_tensor(chosen_w[:], chosen[:],
                                share_s[f][:].unsqueeze(3).to_broadcast(all_), ALU.mult)\
                    .then_inc(comb_step[f], 1)
                dve.wait_ge(comb_step[f], upto(s, 4, 1))
                v.tensor_tensor(comb[:], chosen_w[:, :, 0, :], chosen_w[:, :, 1, :], ALU.add)\
                    .then_inc(comb_step[f], 1)
                dve.wait_ge(comb_step[f], upto(s, 4, 2))
                v.tensor_copy(comb16[:, :, 0:NE], comb[:]).then_inc(comb_step[f], 1)
                dve.wait_ge(comb_step[f], upto(s, 4, 3))
                v.tensor_tensor(comb16[:, :, NE:], comb[:], comb16[:, :, 0:NE], ALU.subtract)\
                    .then_inc(comb_done[f], 1)

            for e in range(NE):
                v.memset(experts[:, :, :, e], float(e))
            for c in range(-1, WAHEAD):
                split_weights(c)
            dve.wait_ge(consts, 4)
            walk(dve, tables["dve"], {
                "gated": gated, "weigh": weigh, "hidden_lo": hidden_lo, "residual": residual,
                "stats": stats, "norm": norm, "x_lo": x_lo, "shift_diff": shift_diff, "mix": mix,
                "mix_lo": mix_lo, "kv": kv, "scan": scan, "bonus": bonus, "receptance": receptance,
                "o_lo": o_lo, "out_residual": out_residual, "top2": top2, "combine": combine})


def kernel(**inputs):
    import numpy as np
    import concourse.bacc as bacc
    from concourse.bass_utils import run_bass_kernel_spmd

    a = {k: np.asarray(v) for k, v in inputs.items()}
    C = a["L0_attn_x"].shape[-1]
    KC = C // P

    def lhs(w):
        return w.T.reshape(KC, P, -1).transpose(1, 0, 2)

    chunks = []
    shared = a["L0_ffn_ws_gate"].shape[0] // P
    for c in range(shared):
        rows = slice(c * P, (c + 1) * P)
        chunks.append((a["L0_ffn_ws_gate"][rows], a["L0_ffn_ws_up"][rows],
                       a["L0_ffn_ws_down"][:, rows]))
    for e in range(a["L0_ffn_w_gate"].shape[0]):
        chunks.append((a["L0_ffn_w_gate"][e], a["L0_ffn_w_up"][e], a["L0_ffn_w_down"][e]))
    w_chunks = np.stack([
        np.concatenate([np.concatenate([lhs(g), lhs(u)], axis=2).reshape(P, -1), d.T], axis=1)
        for g, u, d in chunks])
    w_attn = np.stack([lhs(a[f"L0_attn_{n}"]) for n in ("Wk", "Wv", "Wr", "Wo")], axis=1)
    channels = np.stack([a[f"L0_attn_{n}"].reshape(KC, P).T for n in (
        "time_mix_k", "time_mix_v", "time_mix_r", "time_decay", "time_first", "ln_g", "ln_b")],
        axis=1)
    arrays = {"x": a["L0_attn_x"], "w_chunks": w_chunks, "w_attn": w_attn,
              "w_router": lhs(a["L0_ffn_gate_weight"]), "channels": channels}
    arrays = {f"in_{k}_dram": np.ascontiguousarray(v) for k, v in arrays.items()}

    nc = bacc.Bacc("TRN2", target_bir_lowering=False, num_devices=1)
    args = [nc.dram_tensor(k, v.shape, mybir.dt.from_np(v.dtype), kind="ExternalInput").ap()
            for k, v in arrays.items()]
    out = nc.dram_tensor("out_0_dram", a["L0_attn_x"].shape, F32, kind="ExternalOutput").ap()
    program(nc, *args, out)
    r = run_bass_kernel_spmd(nc, [arrays], core_ids=[0])
    return r.results[0]["out_0_dram"]
```

```python
from contextlib import ExitStack

import concourse.bass as bass
from concourse import mybir

F32 = mybir.dt.float32
F16 = mybir.dt.float16
U32 = mybir.dt.uint32
ALU = mybir.AluOpType
ACT = mybir.ActivationFunctionType

P = 128
EPS = 1e-5
TOPK = 2
ROUTE_SCALE = 2.5
W_SCALE = 256.0
W_UNSCALE = 1.0 / W_SCALE
STEPS = 20
HALF = STEPS // 2


def upto(s, per=1, part=0):
    i, off = s
    return i * per + (off * per + part + 1)


def residuals(phase, s, n_seq):
    i, off = s
    if phase == "A":
        return 2 if isinstance(i, int) and i + off == 0 else i * 4 + off * 4
    return min(4 * (i + off) + 6, 4 * n_seq) if isinstance(i, int) else i * 4 + (off * 4 + 6)


def step_tables(n_chunks, n_shared):
    pe_mid = {0: [("r_proj", -1)], 2: [("scan_turn", -1)], 4: [("turn", -1, "o2")],
              7: [("turn", -1, "3")], 8: [("router", -1, "B")],
              10: [("router_turn", -1, "B"), ("turn", 1, "1")], 12: [("router", 1, "A")],
              16: [("router_turn", 1, "A")]}
    pe_post = {5: [("out_proj", -1)], 13: [("turn", 0, "2")], 17: [("kv_proj", 0, 0)], 18: [("kv_proj", 0, 1)]}

    act_pre = {18: [("k_copy", 0, 0)], 19: [("k_copy", 0, 1)]}
    act_post = {0: [("r_copy", -1, 0), ("r_copy", -1, 1)],
                2: [("o_copy", -1, 0), ("o_copy", -1, 1)],
                4: [("o_affine", -1, 0), ("o_affine", -1, 1), ("o_hi", -1, 0), ("o_hi", -1, 1)],
                7: [("x_hi", -1, "3", 0), ("x_hi", -1, "3", 1)],
                10: [("router_turned", -1, "B"), ("x_hi", 1, "1", 0), ("x_hi", 1, "1", 1)],
                13: [("mix_in", 0, 0), ("mix_in", 0, 1)],
                15: [("mix_hi", 0, 0), ("mix_hi", 0, 1)],
                16: [("router_turned", 1, "A"), ("mix_hi", 0, 2), ("mix_hi", 0, 3)],
                18: [("mix_hi", 0, 4), ("mix_hi", 0, 5)]}

    dve_pre = {0: [("scan", -1, 1)], 1: [("receptance", -1)],
               3: [("stats", -1, "o")], 5: [("o_lo", -1, 0), ("o_lo", -1, 1)],
               6: [("out_residual", -1), ("stats", -1, "3")], 8: [("x_lo", -1, "3", 0), ("x_lo", -1, "3", 1)],
               11: [("x_lo", 1, "1", 0), ("x_lo", 1, "1", 1)],
               12: [("stats", 0, "2")], 14: [("shift_diff", 0)],
               15: [("mix", 0, 0), ("mix", 0, 1)], 16: [("mix", 0, 2), ("mix", 0, 3)],
               17: [("mix_lo", 0, 2), ("mix_lo", 0, 3)],
               18: [("kv", 0, 0), ("mix", 0, 4), ("mix", 0, 5)],
               19: [("kv", 0, 1), ("mix_lo", 0, 4), ("mix_lo", 0, 5)]}
    dve_post = {0: [("bonus", -1, 0), ("bonus", -1, 1)], 1: [("residual", -2, "B")],
                3: [("norm", -1, "o")], 4: [("stats", 1, "1")],                 6: [("norm", -1, "3")], 7: [("norm", 1, "1")],
                8: [("top2", -1, "B")], 9: [("combine", -1, "B")], 11: [("residual", 0, "A")], 12: [("norm", 0, "2"), ("top2", 1, "A")],
                14: [("combine", 1, "A")],
                16: [("mix_lo", 0, 0), ("mix_lo", 0, 1)],
                19: [("scan", 0, 0)]}
    tables = {e: [] for e in ("pe", "act", "dve", "pool", "sp")}
    for k in range(STEPS):
        f, c = ("A", k) if k < HALF else ("B", k - HALF)
        seq = 0 if f == "A" else -1
        back = {n: (("A", k - n, 0) if k - n < HALF else ("B", k - n - HALF, -1)) if k >= n
                else ("B", HALF + k - n, -2) for n in (1, 2)}
        pe = [("gate_up", seq, f, c)]
        pe += pe_mid.get(k, []) + [("down", back[2][2], back[2][0], back[2][1])] + pe_post.get(k, [])
        tables["pe"].append(pe)
        last = (back[1][2], back[1][0], back[1][1])
        tables["act"].append([("hidden_hi", *last)] + act_pre.get(k, []) + [("silu", seq, f, c)]
                             + act_post.get(k, []))
        weigh = [("weigh", seq, f, c)] if c >= n_shared else []
        tables["dve"].append([("hidden_lo", *last)] + dve_pre.get(k, []) + [("gated", seq, f, c)]
                             + weigh + dve_post.get(k, []))
        tables["pool"].append({3: [("rstd", -1, "o")], 4: [("rstd", 1, "1")], 6: [("rstd", -1, "3")],
                               8: [("route_exp", -1, "B")], 12: [("rstd", 0, "2"),
                               ("route_exp", 1, "A")]}.get(k, []))
        tables["sp"].append({1: [("load_norm", 1), ("store", -2)],
                             10: [("spread", -1, "B")], 11: [("load", 1)],
                              16: [("spread", 1, "A")]}.get(k, []))
    return tables


def program(nc, x, w_chunks, w_attn, w_router, channels, comb_dram, out):
    NSEQ, T, C = x.shape
    NCH = w_chunks.shape[0]
    KC = C // P
    NT = T // P
    NE = w_router.shape[2]
    NSH = NCH - NE
    GU = 2 * KC * P
    assert NCH == HALF and T == 512 and C == 256
    MIX_K, MIX_V, MIX_R, DECAY, FIRST, LN_G, LN_B = range(7)

    WAHEAD = 3
    HBUF = 5
    assert NCH % HBUF == 0 and NCH % 2 == 0
    PHASE = {"1": "A", "3": "B"}
    tables = step_tables(NCH, NSH)
    KINDS = {"gate_up": "products", "silu": "values", "gated": "values", "weigh": "values",
             "hidden_hi": "hidden", "hidden_lo": "hidden", "down": "down",
             "residual": "residual"}
    START, STOP, LAST = 1, NSEQ - 2, NSEQ - 1
    BESIDE_FIRST = ([12], [13], [14, 15], [16, 17], [18, 19, 0, 1], [2, 3, 4], [5, 6], [7], [8], [9])
    BESIDE_LAST = ([12], [13], [14, 15], [16, 17], [18, 19, 0, 1], [2, 3], [4], [5], [6], [7, 8, 9])

    def kind(what, off):
        return KINDS.get(what, "prep" if off == 1 else "chain")

    FFN = ("products", "values", "hidden", "down")
    REST = ("residual", "prep", "chain")
    ALL = FFN + REST

    def beside(iteration, first, chain_of, steps_beside, kinds_of):
        order = []
        for c, steps in enumerate(steps_beside):
            order.append((iteration, first + c, ("products",)))
            order += [(chain_of + (k < HALF), k, kinds_of(k)) for k in steps]
            order.append((iteration, first + c, ("values", "hidden", "down")[:c + 1]))
        return order

    prologue = [(-1, k, ALL) for k in range(13)] + [(0, 0, ALL)]
    prologue += [(-1, k, ALL) for k in range(13, STEPS)] + [(0, k, ALL) for k in range(1, HALF)]
    prologue += [(0, 10, ("prep",)), (0, 10, ("hidden", "down")), (0, 11, ("prep",)),
                 (0, 12, ("prep",)), (0, 11, ("down", "residual"))]
    prologue += [(0, k, ("prep",)) for k in range(13, STEPS)]
    prologue += beside(1, 0, 0, BESIDE_FIRST, lambda k: REST if k < HALF else ("chain",))
    epilogue = [(STOP, k, ALL) for k in range(HALF, STEPS)] + [(LAST, k, ALL) for k in range(HALF)]
    epilogue += [(LAST, 10, ("hidden", "down", "chain")), (LAST, 11, ("down", "residual"))]
    epilogue += beside(LAST, HALF, LAST, BESIDE_LAST, lambda k: REST if k != 1 else ("prep", "chain"))
    epilogue += [(LAST + 1, 0, ("hidden", "down")), (LAST + 1, 1, ("down", "residual"))]
    epilogue += [(LAST + 1, k, ALL) for k in range(HALF, STEPS)]
    epilogue += [(LAST + 2, k, ALL) for k in range(2)]
    loop = [(0, k) for k in range(HALF, STEPS)] + [(1, k) for k in range(HALF)]

    def live(i, off):
        return not isinstance(i, int) or 0 <= i + off < NSEQ

    def walk(eng, table, do):
        def steps(some):
            for i, k, kinds in some:
                for what, off, *args in table[k]:
                    if live(i, off) and kind(what, off) in kinds:
                        do[what]((i, off), *args)
        steps(prologue)
        with eng.Fori(START, STOP) as i:
            for later, k in loop:
                for what, off, *args in table[k]:
                    do[what]((i, off + later), *args)
        steps(epilogue)

    def whole_stream(table):
        order = prologue + [(i + later, k, ALL) for i in range(START, STOP) for later, k in loop]
        for i, k, kinds in order + epilogue:
            for what, off, *args in table[k]:
                if live(i, off) and kind(what, off) in kinds:
                    yield what, i + off, args

    OUT_BANK, RING = 0, (2, 3, 4, 5, 6, 7)
    USES = {"gate_up": 2, "turn": 2, "scan_turn": 2, "out_proj": 2, "kv_proj": 2, "r_proj": 2,
            "router": 1, "router_turn": 1}
    PASSED = {"router_turn": 2}
    banks, before, held = {}, {}, {}
    n_ring = 0
    for what, seq, args in whole_stream(tables["pe"]):
        for b in range(USES.get(what, 0)):
            bank = RING[n_ring % len(RING)]
            n_ring += 1
            banks[what, *args, b, seq] = bank
            if bank in held:
                t, s = held[bank]
                before[what, *args, b, seq] = (t, s - seq)
            held[bank] = ((what, *args, b), seq)
        n_ring += PASSED.get(what, 0)
    IN_LOOP = NSEQ // 2
    for later, k in loop:
        for what, off, *args in tables["pe"][k]:
            for b in range(USES.get(what, 0)):
                assert len({before[what, *args, b, i + later + off] for i in range(START, STOP)}) == 1
    assert all(banks[t] == banks[*t[:-1], IN_LOOP + 1] and before[t] == before[*t[:-1], IN_LOOP + 1]
               for t in banks if t[-1] == IN_LOOP)

    def at(s):
        i, off = s
        return i + off if isinstance(i, int) else IN_LOOP

    def bank_of(s, *task_b):
        return banks[*task_b, at(s)]

    with ExitStack() as ctx:
        def sb(name, shape, dt=F32):
            return ctx.enter_context(nc.sbuf_tensor(name, shape, dt))

        def sem(name):
            return ctx.enter_context(nc.semaphore(name))

        ps = ctx.enter_context(nc.psum_tensor("ps", [P, 8, 512], F32))

        w_hi = sb("w_hi", [P, NCH, GU + C], F16)
        w_lo = sb("w_lo", [P, NCH, GU + C], F16)
        a_hi = sb("a_hi", [P, 4, KC, C], F16)
        a_lo = sb("a_lo", [P, 4, KC, C], F16)
        r_hi = sb("r_hi", [P, KC, NE], F16)
        r_lo = sb("r_lo", [P, KC, NE], F16)
        r_stage = sb("r_stage", [P, KC, NE])
        chan = sb("chan", [P, 7, KC])
        decay = sb("decay", [P, KC])
        arena = sb("arena", [P, NCH * (GU + C) + 4 * KC * C])
        w_stage = arena[:, 0:NCH * (GU + C)].rearrange("p (c n) -> p c n", c=NCH)
        a_stage = arena[:, NCH * (GU + C):].rearrange("p (a k n) -> p a k n", a=4, k=KC)
        mix32 = arena[:, 0:6 * T].rearrange("p (j t) -> p j t", j=6)

        def tile_at(n):
            return arena[:, (6 + 2 * n) * T:(8 + 2 * n) * T].rearrange("p (m t) -> p m t", m=KC)

        diff, k_sb, kv_sb, state, r_sb, o_aff = (tile_at(n) for n in range(6))

        ident = sb("ident", [P, P])
        experts = sb("experts", [P, NT, TOPK, NE])
        neg_half = sb("neg_half", [P, NT])
        inv_e = sb("inv_e", [P, NT, TOPK])
        euler = sb("euler", [P, KC])
        eps_t = sb("eps_t", [P, NT])

        x0 = sb("x0", [P, NT, C])
        x_norm = sb("x_norm", [P, NT, C])
        x1 = sb("x1", [P, NT, C])
        x2 = sb("x2", [P, NT, C])
        x3 = sb("x3", [P, NT, C])
        o_tok = sb("o_tok", [P, NT, C])
        LNS = ("1", "2", "o", "3")
        normed = {n: sb(f"normed{n}", [P, NT, C]) for n in ("1", "2", "3")} | {"o": o_tok}
        ln_in = {"1": x_norm, "2": x1, "o": o_tok}
        stat = {n: sb(f"stat{n}", [P, NT, 6]) for n in LNS}
        mean_var = {n: sb(f"mean_var{n}", [P, NT, 2]) for n in LNS}
        var_eps = {n: sb(f"var_eps{n}", [P, NT]) for n in LNS}
        rstd_t = {n: sb(f"rstd{n}", [P, NT]) for n in LNS}

        xh = {f: sb(f"xh{f}", [P, KC, T], F16) for f in "AB"}
        xl = {f: sb(f"xl{f}", [P, KC, T], F16) for f in "AB"}
        shifted = sb("shifted", [P, KC, T + 1])
        mix_h = sb("mix_h", [P, 6, T], F16)
        mix_l = sb("mix_l", [P, 6, T], F16)
        oh = sb("oh", [P, KC, T], F16)
        ol = sb("ol", [P, KC, T], F16)

        silu_t = sb("silu_t", [P, 2, T])
        gated_t = sb("gated_t", [P, 2, T])
        hid = sb("hid", [P, 2, T])
        hid_h = sb("hid_h", [P, HBUF, T], F16)
        hid_l = sb("hid_l", [P, HBUF, T], F16)

        logits = {f: sb(f"logits{f}", [P, NT, NE]) for f in "AB"}
        best = {f: sb(f"best{f}", [P, NT, NE]) for f in "AB"}
        best_at = {f: sb(f"best_at{f}", [P, NT, NE], U32) for f in "AB"}
        p_exp = {f: sb(f"p_exp{f}", [P, NT, TOPK]) for f in "AB"}
        p_one = sb("p_one", [P, NT, TOPK])
        score = sb("score", [P, NT, TOPK])
        score_sum = sb("score_sum", [P, NT])
        score_eps = sb("score_eps", [P, NT])
        score_inv = sb("score_inv", [P, NT])
        share = sb("share", [P, NT, TOPK])
        chosen = sb("chosen", [P, NT, TOPK, NE])
        chosen_w = sb("chosen_w", [P, NT, TOPK, NE])
        comb = sb("comb", [P, NT, NE])
        comb_t = {f: sb(f"comb_t{f}", [NE, T]) for f in "AB"}
        AT_ONCE = 2
        spread_t = {f: sb(f"spread_t{f}", [P, NE, T]) for f in "AB"}

        w_in = [sem(f"w_in{c}") for c in range(NCH)]
        attn_in, router_in, chan_in = sem("attn_in"), sem("router_in"), sem("chan_in")
        x_in, x_norm_in, stored = sem("x_in"), sem("x_norm_in"), sem("stored")
        w_hi_done, w_split = sem("w_hi_done"), sem("w_split")
        const_set, consts = sem("const_set"), sem("consts")
        gate_done = {f: sem(f"gate_done{f}") for f in "AB"}
        up_done = {f: sem(f"up_done{f}") for f in "AB"}
        down_done = {f: sem(f"down_done{f}") for f in "AB"}
        comb_out = {f: sem(f"comb_out{f}") for f in "AB"}
        spread_in = {f: [sem(f"spread_in{f}{q}") for q in range(NE // AT_ONCE)] for f in "AB"}
        silu_done = {f: sem(f"silu_done{f}") for f in "AB"}
        gated_done = {f: sem(f"gated_done{f}") for f in "AB"}
        weigh_done = {f: sem(f"weigh_done{f}") for f in "AB"}
        hi_done = {f: sem(f"hi_done{f}") for f in "AB"}
        lo_done = {f: sem(f"lo_done{f}") for f in "AB"}
        residual_done, x2_done = sem("residual_done"), sem("x2_done")
        stats_done = {n: sem(f"stats_done{n}") for n in LNS}
        moments_done = {n: sem(f"moments_done{n}") for n in LNS}
        var_done = {n: sem(f"var_done{n}") for n in LNS}
        rstd_done = {n: sem(f"rstd_done{n}") for n in LNS}
        norm_done = {n: sem(f"norm_done{n}") for n in LNS}
        turned = {n: sem(f"turned{n}") for n in ("1", "2", "o2", "3")}
        turned_hi = {n: sem(f"turned_hi{n}") for n in ("1", "3")}
        turned_lo = {n: sem(f"turned_lo{n}") for n in ("1", "3")}
        mix_in_done, diff_done = sem("mix_in_done"), sem("diff_done")
        mix_done, mix_hi_done, mix_lo_done = sem("mix_done"), sem("mix_hi_done"), sem("mix_lo_done")
        k_done, v_done, r_done = sem("k_done"), sem("v_done"), sem("r_done")
        k_copied, r_copied = sem("k_copied"), sem("r_copied")
        kv_done, scan_done, bonus_done = sem("kv_done"), sem("scan_done"), sem("bonus_done")
        mixed_done, scan_turned, o_copied = sem("mixed_done"), sem("scan_turned"), sem("o_copied")
        o_affine_done, o_hi_done, o_lo_done = sem("o_affine_done"), sem("o_hi_done"), sem("o_lo_done")
        out_proj_done = sem("out_proj_done")
        router_done = {f: sem(f"router_done{f}") for f in "AB"}
        logits_out = {f: sem(f"logits_out{f}") for f in "AB"}
        max_done = {f: sem(f"max_done{f}") for f in "AB"}
        top2_done = {f: sem(f"top2_done{f}") for f in "AB"}
        exp_done = {f: sem(f"exp_done{f}") for f in "AB"}
        comb_step = {f: sem(f"comb_step{f}") for f in "AB"}
        comb_done = {f: sem(f"comb_done{f}") for f in "AB"}
        comb_turned = {f: sem(f"comb_turned{f}") for f in "AB"}
        comb_copied = {f: sem(f"comb_copied{f}") for f in "AB"}

        def x2_of(s):
            return x_norm if at(s) == LAST else x2

        def own_wait(eng, signal, value):
            eng.wait_ge(consts, 2)
            eng.wait_ge(signal, value)

        def silu_before(s, f, c):
            i, off = s
            if c >= 2:
                return s, f, c - 2
            prev, other = ((i, off - 2), "B") if f == "A" else ((i, off + 1), "A")
            if live(i, prev[1]):
                return prev, other, c + NCH - 2
            return ((i, off - 1), f, c + NCH - 2) if live(i, off - 1) else (None, f, c)

        def released(task, s):
            what, *args, b = task
            if what == "gate_up":
                f, c = args
                return (silu_done, gated_done)[b][f], upto(s, NCH, c)
            if what == "turn":
                n = args[0]
                if n == "2":
                    return mix_in_done, upto(s, KC, b)
                if n == "o2":
                    return o_affine_done, upto(s, KC, b)
                return turned_lo[n], upto(s, KC, b)
            if what == "scan_turn":
                return o_copied, upto(s, 2, b)
            if what == "out_proj":
                return x2_done, upto(s, 2, b)
            if what == "kv_proj":
                return (k_copied, kv_done)[b], upto(s, KC, args[0])
            if what == "r_proj":
                return r_copied, upto(s, KC, b)
            if what == "router":
                return logits_out[args[0]], upto(s)
            return comb_copied[args[0]], upto(s)

        block = ctx.enter_context(nc.Block())

        @block.sync
        def _(sp):
            x_tok = x.rearrange("s (j p) c -> s p j c", p=P)
            out_tok = out.rearrange("s (j p) c -> s p j c", p=P)

            def load_next(s):
                i, off = s
                if isinstance(i, int) and i + off == 0:
                    return
                sp.wait_ge(residual_done, residuals("A", (i, off - 1), NSEQ))
                sp.dma_start(x0[:], x_tok[i + off]).then_inc(x_in, 16)

            def store(s):
                i, off = s
                sp.wait_ge(residual_done, residuals("B", s, NSEQ))
                sp.dma_start(out_tok[i + off], x3[:]).then_inc(stored, 16)

            def load_norm(s):
                i, off = s
                if isinstance(i, int) and i + off == 0:
                    return
                sp.wait_ge(norm_done["1"], i + off)
                sp.dma_start(x_norm[:], x_tok[i + off]).then_inc(x_norm_in, 16)

            def spread(s, f):
                sp.wait_ge(comb_copied[f], upto(s))
                sp.dma_start(comb_dram[f], comb_t[f][:]).then_inc(comb_out[f], 16)
                sp.wait_ge(comb_out[f], upto(s, 16, 15))
                for q in range(NE // AT_ONCE):
                    some = slice(q * AT_ONCE, (q + 1) * AT_ONCE)
                    sp.dma_start(spread_t[f][:, some, :], comb_dram[f][some, :].partition_broadcast(P))\
                        .then_inc(spread_in[f][q], 16)

            sp.dma_start(x_norm[:], x_tok[0]).then_inc(x_norm_in, 16)
            sp.dma_start(r_stage[:], w_router).then_inc(router_in, 16)
            for c in range(0, NCH):
                sp.dma_start(w_stage[:, c, :], w_chunks[c]).then_inc(w_in[c], 16)
            sp.dma_start(x0[:], x_tok[0]).then_inc(x_in, 16)
            sp.dma_start(a_stage, w_attn).then_inc(attn_in, 16)
            walk(sp, tables["sp"], {"load": load_next, "load_norm": load_norm, "store": store,
                                    "spread": spread})
            sp.wait_ge(stored, 16 * NSEQ)

        @block.gpsimd
        def _(pool):
            g = nc.gpsimd
            g.memset(ident[:], 0.0).then_inc(const_set, 1)
            g.memset(neg_half[:], -0.5).then_inc(const_set, 1)
            g.memset(inv_e[:], 0.36787944117144233).then_inc(const_set, 1)
            g.memset(euler[:], 2.718281828459045).then_inc(const_set, 1)
            g.memset(shifted[:, :, 0:1], 0.0).then_inc(const_set, 1)
            g.memset(eps_t[:], EPS).then_inc(const_set, 1)
            pool.wait_ge(const_set, 6)
            g.affine_select(out=ident[:], in_=ident[:], compare_op=ALU.not_equal, fill=1.0, base=0,
                            pattern=[[-1, P]], channel_multiplier=1).then_inc(consts, 1)
            pool.wait_ge(chan_in, 16)
            g.tensor_tensor(decay[:], euler[:], chan[:, DECAY, :], ALU.pow).then_inc(consts, 1)

            def rstd(s, n):
                pool.wait_ge(moments_done[n], upto(s))
                g.tensor_tensor(var_eps[n][:], mean_var[n][:, :, 1], eps_t[:], ALU.add)\
                    .then_inc(var_done[n], 1)
                pool.wait_ge(var_done[n], upto(s))
                g.tensor_tensor(rstd_t[n][:], var_eps[n][:], neg_half[:], ALU.pow)\
                    .then_inc(rstd_done[n], 1)

            def route_exp(s, f):
                pool.wait_ge(top2_done[f], upto(s))
                g.tensor_tensor(p_exp[f][:], inv_e[:], best[f][:, :, 0:TOPK], ALU.pow)\
                    .then_inc(exp_done[f], 1)

            walk(pool, tables["pool"], {"rstd": rstd, "route_exp": route_exp})

        @block.tensor
        def _(pe):
            def bank_free(s, *task_b):
                if (*task_b, at(s)) in before:
                    task, rel = before[(*task_b, at(s))]
                    pe.wait_ge(*released(task, (s[0], s[1] + rel)))
                return bank_of(s, *task_b)

            def three(out_ap, hi_w, lo_w, hi_x, lo_x, first, last, lone):
                nc.tensor.matmul(out_ap, hi_w, hi_x, start=first, stop=False, skip_group_check=lone)
                nc.tensor.matmul(out_ap, lo_w, hi_x, start=False, stop=False, skip_group_check=lone)
                return nc.tensor.matmul(out_ap, hi_w, lo_x, start=False, stop=last,
                                        skip_group_check=lone)

            def gate_up(s, f, c):
                i, off = s
                if c == 0:
                    pe.wait_ge(turned_lo["1" if f == "A" else "3"], upto(s, KC, KC - 1))
                if f == "A" and isinstance(i, int) and i + off == 0:
                    pe.wait_ge(w_split, c + 2)
                for b, done in ((0, gate_done), (1, up_done)):
                    bank = bank_free(s, "gate_up", f, c, b)
                    for k in range(KC):
                        cols = slice(k * 2 * P + b * P, k * 2 * P + (b + 1) * P)
                        mm = three(ps[:, bank, :], w_hi[:, c, cols], w_lo[:, c, cols],
                                   xh[f][:, k, :], xl[f][:, k, :], k == 0, k == KC - 1, False)
                    mm.then_inc(done[f], 1)

            def down(s, f, c):
                i, off = s
                pe.wait_ge(lo_done[f], upto(s, NCH, c))
                if c == 0 and not (f == "A" and isinstance(i, int) and i + off == 0):
                    if f == "A":
                        pe.wait_ge(residual_done, i * 4 + (off * 4 - 2))
                    else:
                        v = i * 4 + (off * 4 + 4)
                        pe.wait_ge(residual_done, min(v, 4 * NSEQ - 2) if isinstance(i, int) else v)
                b = c % HBUF
                for j in range(NT):
                    tok = slice(j * P, (j + 1) * P)
                    half = ps[:, OUT_BANK + j // 2, (j % 2) * C:(j % 2 + 1) * C]
                    wh, wl = w_hi[:, c, GU:], w_lo[:, c, GU:]
                    nc.tensor.matmul(half, hid_h[:, b, tok], wh, start=(c == 0 and j % 2 == 0),
                                     stop=False, skip_group_check=True)
                    nc.tensor.matmul(half, hid_h[:, b, tok], wl, start=False, stop=False,
                                     skip_group_check=True)
                    mm = nc.tensor.matmul(half, hid_l[:, b, tok], wh, start=False,
                                          stop=(c == NCH - 1 and j % 2 == 1), skip_group_check=True)
                mm.then_inc(down_done[f], 1)

            def turn(s, n):
                pe.wait_ge(norm_done[n[0]], upto(s))
                for m in range(KC):
                    bank = bank_free(s, "turn", n, m)
                    for j in range(NT):
                        mm = nc.tensor.transpose(ps[:, bank, j * P:(j + 1) * P],
                                                 normed[n[0]][:, j, m * P:(m + 1) * P], ident[:])
                    mm.then_inc(turned[n], 1)

            def kv_proj(s, m):
                if m == 0 and at(s) == 0:
                    pe.wait_ge(w_split, NCH + 2)
                for b, done in ((0, k_done), (1, v_done)):
                    if m == 0:
                        pe.wait_ge(mix_lo_done, upto(s, 6, b * KC + KC - 1))
                    bank = bank_free(s, "kv_proj", m, b)
                    project(bank, b, m).then_inc(done, 1)

            def project(bank, which, m):
                for k in range(KC):
                    cols = slice(m * P, (m + 1) * P)
                    mm = three(ps[:, bank, :], a_hi[:, which, k, cols], a_lo[:, which, k, cols],
                               mix_h[:, which * KC + k, :], mix_l[:, which * KC + k, :],
                               k == 0, k == KC - 1, False)
                return mm

            def r_proj(s):
                pe.wait_ge(mix_lo_done, upto(s, 6, 5))
                for m in range(KC):
                    bank = bank_free(s, "r_proj", m)
                    project(bank, 2, m).then_inc(r_done, 1)

            def scan_turn(s):
                pe.wait_ge(mixed_done, upto(s))
                for b in range(2):
                    bank = bank_free(s, "scan_turn", b)
                    for j in range(2):
                        for m in range(KC):
                            t0 = (2 * b + j) * P
                            mm = nc.tensor.transpose(ps[:, bank, j * C + m * P:j * C + (m + 1) * P],
                                                     state[:, m, t0:t0 + P], ident[:])
                    mm.then_inc(scan_turned, 1)

            def out_proj(s):
                pe.wait_ge(o_lo_done, upto(s, KC, KC - 1))
                for b in range(2):
                    bank = bank_free(s, "out_proj", b)
                    for j in range(2):
                        tok = slice((2 * b + j) * P, (2 * b + j + 1) * P)
                        half = ps[:, bank, j * C:(j + 1) * C]
                        for k in range(KC):
                            nc.tensor.matmul(half, oh[:, k, tok], a_hi[:, 3, k, :],
                                             start=(k == 0 and j == 0), stop=False,
                                             skip_group_check=True)
                            nc.tensor.matmul(half, oh[:, k, tok], a_lo[:, 3, k, :], start=False,
                                             stop=False, skip_group_check=True)
                            mm = nc.tensor.matmul(half, ol[:, k, tok], a_hi[:, 3, k, :], start=False,
                                                  stop=(k == KC - 1 and j == 1),
                                                  skip_group_check=True)
                    mm.then_inc(out_proj_done, 1)

            def router(s, f):
                pe.wait_ge(turned_lo["1" if f == "A" else "3"], upto(s, KC, KC - 1))
                if f == "A" and isinstance(s[0], int) and sum(s) == 0:
                    pe.wait_ge(w_split, 1)
                bank = bank_free(s, "router", f, 0)
                for j in range(NT):
                    tok = slice(j * P, (j + 1) * P)
                    cell = ps[:, bank, j * NE:(j + 1) * NE]
                    for k in range(KC):
                        nc.tensor.matmul(cell, xh[f][:, k, tok], r_hi[:, k, :],
                                         start=(j == 0 and k == 0), stop=False, skip_group_check=True)
                        nc.tensor.matmul(cell, xh[f][:, k, tok], r_lo[:, k, :], start=False,
                                         stop=False, skip_group_check=True)
                        mm = nc.tensor.matmul(cell, xl[f][:, k, tok], r_hi[:, k, :], start=False,
                                              stop=(j == NT - 1 and k == KC - 1),
                                              skip_group_check=True)
                mm.then_inc(router_done[f], 1)

            def router_turn(s, f):
                pe.wait_ge(comb_done[f], upto(s))
                bank = bank_free(s, "router_turn", f, 0)
                for j in range(NT):
                    mm = nc.tensor.transpose(ps[0:NE, bank, j * P:(j + 1) * P], comb[:, j, :],
                                             ident[:])
                mm.then_inc(comb_turned[f], 1)

            pe.wait_ge(consts, 1)
            walk(pe, tables["pe"], {
                "gate_up": gate_up, "down": down, "turn": turn,
                "kv_proj": kv_proj, "r_proj": r_proj, "scan_turn": scan_turn, "out_proj": out_proj,
                "router": router, "router_turn": router_turn})

        @block.scalar
        def _(act):
            act.dma_start(chan[:], channels).then_inc(chan_in, 16)

            def split_weights(c):
                if c < 0:
                    act.wait_ge(router_in, 16)
                    nc.scalar.activation(r_hi[:], r_stage[:], ACT.Copy, scale=W_SCALE)\
                        .then_inc(w_hi_done, 1)
                elif c < NCH:
                    act.wait_ge(w_in[c], 16)
                    nc.scalar.activation(w_hi[:, c, :], w_stage[:, c, :], ACT.Copy, scale=W_SCALE)\
                        .then_inc(w_hi_done, 1)
                else:
                    act.wait_ge(attn_in, 16)
                    nc.scalar.activation(a_hi[:], a_stage, ACT.Copy, scale=W_SCALE)\
                        .then_inc(w_hi_done, 1)

            def silu(s, f, c):
                if f == "A" and isinstance(s[0], int) and sum(s) == 0:
                    if c + WAHEAD <= NCH:
                        split_weights(c + WAHEAD)
                act.wait_ge(gate_done[f], upto(s, NCH, c))
                last, lf, lc = silu_before(s, f, c)
                if last is not None:
                    act.wait_ge(gated_done[lf], upto(last, NCH, lc))
                nc.scalar.activation(silu_t[:, c % 2, :], ps[:, bank_of(s, "gate_up", f, c, 0), :],
                                     ACT.Silu, scale=W_UNSCALE).then_inc(silu_done[f], 1)

            def hidden_hi(s, f, c):
                if c < NSH:
                    act.wait_ge(gated_done[f], upto(s, NCH, c))
                else:
                    act.wait_ge(weigh_done[f], upto(s, NE, c - NSH))
                b = c % HBUF
                nc.scalar.copy(hid_h[:, b, :], hid[:, c % 2, :]).then_inc(hi_done[f], 1)

            def x_hi(s, n, m):
                act.wait_ge(turned[n], upto(s, KC, m))
                nc.scalar.copy(xh[PHASE[n]][:, m, :], ps[:, bank_of(s, "turn", n, m), :])\
                    .then_inc(turned_hi[n], 1)

            def mix_in(s, m):
                act.wait_ge(turned["2"], upto(s, KC, m))
                nc.scalar.copy(shifted[:, m, 1:T + 1], ps[:, bank_of(s, "turn", "2", m), :])\
                    .then_inc(mix_in_done, 1)

            def mix_hi(s, j):
                act.wait_ge(mix_done, upto(s, 6, j))
                nc.scalar.copy(mix_h[:, j, :], mix32[:, j, :]).then_inc(mix_hi_done, 1)

            def k_copy(s, m):
                act.wait_ge(k_done, upto(s, KC, m))
                nc.scalar.activation(k_sb[:, m, :], ps[:, bank_of(s, "kv_proj", m, 0), :], ACT.Copy,
                                     scale=W_UNSCALE).then_inc(k_copied, 1)

            def r_copy(s, m):
                act.wait_ge(r_done, upto(s, KC, m))
                nc.scalar.activation(r_sb[:, m, :], ps[:, bank_of(s, "r_proj", m), :], ACT.Copy,
                                     scale=W_UNSCALE).then_inc(r_copied, 1)

            def o_copy(s, b):
                act.wait_ge(scan_turned, upto(s, 2, b))
                nc.scalar.copy(o_tok[:, 2 * b:2 * b + 2, :],
                               ps[:, bank_of(s, "scan_turn", b), :].rearrange("p (j c) -> p j c", j=2))\
                    .then_inc(o_copied, 1)

            def o_affine(s, m):
                act.wait_ge(turned["o2"], upto(s, KC, m))
                nc.scalar.activation(o_aff[:, m, :], ps[:, bank_of(s, "turn", "o2", m), :], ACT.Identity,
                                     bias=chan[:, LN_B, m:m + 1], scale=chan[:, LN_G, m:m + 1])\
                    .then_inc(o_affine_done, 1)

            def o_hi(s, m):
                act.wait_ge(o_affine_done, upto(s, KC, m))
                nc.scalar.copy(oh[:, m, :], o_aff[:, m, :]).then_inc(o_hi_done, 1)

            def router_turned(s, f):
                act.wait_ge(comb_turned[f], upto(s))
                nc.scalar.copy(comb_t[f][:], ps[0:NE, bank_of(s, "router_turn", f, 0), :])\
                    .then_inc(comb_copied[f], 1)

            act.wait_ge(consts, 1)
            nc.scalar.activation(silu_t[:, 1, 0:1], ident[:, 0:1], ACT.Silu)
            for c in range(-1, WAHEAD):
                split_weights(c)
            act.wait_ge(chan_in, 16)
            walk(act, tables["act"], {
                "silu": silu, "hidden_hi": hidden_hi, "x_hi": x_hi, "mix_in": mix_in,
                "mix_hi": mix_hi, "k_copy": k_copy, "r_copy": r_copy, "o_copy": o_copy,
                "o_affine": o_affine, "o_hi": o_hi, "router_turned": router_turned})

        @block.vector
        def _(dve):
            v = nc.vector

            def split_weights(c):
                dve.wait_ge(w_hi_done, c + 2)
                if c < 0:
                    hi, lo, full = r_hi[:], r_lo[:], r_stage[:]
                elif c < NCH:
                    hi, lo, full = w_hi[:, c, :], w_lo[:, c, :], w_stage[:, c, :]
                else:
                    flat = "p a k n -> p (a k n)"
                    hi, lo, full = (a_hi[:].rearrange(flat), a_lo[:].rearrange(flat),
                                    a_stage.rearrange(flat))
                v.scalar_tensor_tensor(out=lo, in0=full, scalar=W_SCALE, in1=hi, op0=ALU.mult,
                                       op1=ALU.subtract).then_inc(w_split, 1)

            def gated(s, f, c):
                if f == "A" and isinstance(s[0], int) and sum(s) == 0:
                    if c + WAHEAD <= NCH:
                        split_weights(c + WAHEAD)
                dve.wait_ge(silu_done[f], upto(s, NCH, c))
                dve.wait_ge(up_done[f], upto(s, NCH, c))
                to = hid if c < NSH else gated_t
                v.scalar_tensor_tensor(out=to[:, c % 2, :], in0=ps[:, bank_of(s, "gate_up", f, c, 1), :],
                                       scalar=W_UNSCALE, in1=silu_t[:, c % 2, :], op0=ALU.mult,
                                       op1=ALU.mult).then_inc(gated_done[f], 1)

            def weigh(s, f, c):
                dve.wait_ge(gated_done[f], upto(s, NCH, c))
                dve.wait_ge(spread_in[f][(c - NSH) // AT_ONCE], upto(s, 16, 15))
                v.tensor_tensor(hid[:, c % 2, :], gated_t[:, c % 2, :],
                                spread_t[f][:, c - NSH, :], ALU.mult)\
                    .then_inc(weigh_done[f], 1)

            def hidden_lo(s, f, c):
                dve.wait_ge(hi_done[f], upto(s, NCH, c))
                b = c % HBUF
                v.tensor_tensor(hid_l[:, b, :], hid[:, c % 2, :], hid_h[:, b, :], ALU.subtract)\
                    .then_inc(lo_done[f], 1)

            def residual(s, f):
                i, off = s
                dve.wait_ge(down_done[f], upto(s, NCH, NCH - 1))
                if f == "A":
                    dve.wait_ge(x_in, upto(s, 16, 15))
                else:
                    dve.wait_ge(x2_done, upto(s, 2, 1))
                    if not (isinstance(i, int) and i + off == 0):
                        dve.wait_ge(stored, i * 16 + off * 16)
                src, dst = (x0, x1) if f == "A" else (x2_of(s), x3)
                for b in range(2):
                    v.scalar_tensor_tensor(
                        out=dst[:, 2 * b:2 * b + 2, :].rearrange("p j c -> p (j c)"),
                        in0=ps[:, OUT_BANK + b, :], scalar=0.5 * W_UNSCALE,
                        in1=src[:, 2 * b:2 * b + 2, :].rearrange("p j c -> p (j c)"),
                        op0=ALU.mult, op1=ALU.add).then_inc(residual_done, 1)

            def stats(s, n):
                of_all = upto(s) if isinstance(s[0], int) else dve.to_reg(upto(s))
                if n == "1":
                    dve.wait_ge(x_norm_in, upto(s, 16, 15))
                elif n == "2":
                    dve.wait_ge(residual_done, residuals("A", s, NSEQ))
                elif n == "o":
                    dve.wait_ge(o_copied, upto(s, 2, 1))
                else:
                    dve.wait_ge(x2_done, upto(s, 2, 1))
                x_in_ln = x2_of(s) if n == "3" else ln_in[n]
                for j in range(NT):
                    ins = v.bn_stats(out=stat[n][:, j, :], in_=x_in_ln[:, j, :])
                ins.then_inc(stats_done[n], 1)
                own_wait(dve, stats_done[n], of_all)
                for j in range(NT):
                    ins = v.bn_aggr(out=mean_var[n][:, j, :], in_=stat[n][:, j, :])
                ins.then_inc(moments_done[n], 1)

            def norm(s, n):
                if n == "1" and at(s) == 0:
                    for c in range(-1, 1):
                        split_weights(c)
                dve.wait_ge(moments_done[n], upto(s))
                dve.wait_ge(rstd_done[n], upto(s))
                x_in_ln = x2_of(s) if n == "3" else ln_in[n]
                for j in range(NT):
                    ins = v.tensor_scalar(normed[n][:, j, :], x_in_ln[:, j, :],
                                          mean_var[n][:, j, 0:1], rstd_t[n][:, j:j + 1],
                                          ALU.subtract, ALU.mult)
                ins.then_inc(norm_done[n], 1)
                if n == "1" and at(s) == 0:
                    for c in range(1, WAHEAD):
                        split_weights(c)

            def x_lo(s, n, m):
                dve.wait_ge(turned_hi[n], upto(s, KC, m))
                v.tensor_tensor(xl[PHASE[n]][:, m, :], ps[:, bank_of(s, "turn", n, m), :],
                                xh[PHASE[n]][:, m, :], ALU.subtract).then_inc(turned_lo[n], 1)

            def shift_diff(s):
                dve.wait_ge(mix_in_done, upto(s, KC, KC - 1))
                v.tensor_tensor(diff, shifted[:, :, 1:T + 1], shifted[:, :, 0:T], ALU.subtract)\
                    .then_inc(diff_done, 1)

            def mix(s, j):
                which, m = divmod(j, KC)
                dve.wait_ge(diff_done, upto(s))
                v.scalar_tensor_tensor(out=mix32[:, j, :], in0=diff[:, m, :],
                                       scalar=chan[:, MIX_K + which, m:m + 1],
                                       in1=shifted[:, m, 0:T], op0=ALU.mult, op1=ALU.add)\
                    .then_inc(mix_done, 1)

            def mix_lo(s, j):
                dve.wait_ge(mix_hi_done, upto(s, 6, j))
                v.tensor_tensor(mix_l[:, j, :], mix32[:, j, :], mix_h[:, j, :], ALU.subtract)\
                    .then_inc(mix_lo_done, 1)

            def kv(s, m):
                dve.wait_ge(k_copied, upto(s, KC, m))
                dve.wait_ge(v_done, upto(s, KC, m))
                v.scalar_tensor_tensor(out=kv_sb[:, m, :], in0=ps[:, bank_of(s, "kv_proj", m, 1), :],
                                       scalar=W_UNSCALE, in1=k_sb[:, m, :], op0=ALU.mult,
                                       op1=ALU.mult).then_inc(kv_done, 1)

            def scan(s, m):
                dve.wait_ge(kv_done, upto(s, KC, m))
                v.tensor_tensor_scan(state[:, m, :], decay[:, m:m + 1].to_broadcast([P, T]),
                                     kv_sb[:, m, :], 0.0, ALU.mult, ALU.add).then_inc(scan_done, 1)

            def bonus(s, m):
                dve.wait_ge(scan_done, upto(s, KC, m))
                v.scalar_tensor_tensor(out=state[:, m, :], in0=kv_sb[:, m, :],
                                       scalar=chan[:, FIRST, m:m + 1], in1=state[:, m, :],
                                       op0=ALU.mult, op1=ALU.add).then_inc(bonus_done, 1)

            def receptance(s):
                dve.wait_ge(bonus_done, upto(s, KC, KC - 1))
                dve.wait_ge(r_copied, upto(s, KC, KC - 1))
                v.tensor_tensor(state, state, r_sb, ALU.mult).then_inc(mixed_done, 1)

            def o_lo(s, m):
                dve.wait_ge(o_hi_done, upto(s, KC, m))
                v.tensor_tensor(ol[:, m, :], o_aff[:, m, :], oh[:, m, :], ALU.subtract)\
                    .then_inc(o_lo_done, 1)

            def out_residual(s):
                for b in range(2):
                    dve.wait_ge(out_proj_done, upto(s, 2, b))
                    v.scalar_tensor_tensor(
                        out=x2_of(s)[:, 2 * b:2 * b + 2, :].rearrange("p j c -> p (j c)"),
                        in0=ps[:, bank_of(s, "out_proj", b), :], scalar=W_UNSCALE,
                        in1=x1[:, 2 * b:2 * b + 2, :].rearrange("p j c -> p (j c)"),
                        op0=ALU.mult, op1=ALU.add).then_inc(x2_done, 1)

            def top2(s, f):
                dve.wait_ge(router_done[f], upto(s))
                v.tensor_scalar(logits[f][:].rearrange("p j e -> p (j e)"),
                                ps[:, bank_of(s, "router", f, 0), 0:NT * NE], W_UNSCALE, None, ALU.mult)\
                    .then_inc(logits_out[f], 1)
                own_wait(dve, logits_out[f], upto(s))
                for j in range(NT):
                    ins = v.max(out=best[f][:, j, :], in_=logits[f][:, j, :])
                ins.then_inc(max_done[f], 1)
                own_wait(dve, max_done[f], upto(s))
                for j in range(NT):
                    ins = v.max_index(out=best_at[f][:, j, :], in_max=best[f][:, j, :],
                                      in_values=logits[f][:, j, :])
                ins.then_inc(top2_done[f], 1)

            def combine(s, f):
                all_ = [P, NT, TOPK, NE]
                dve.wait_ge(exp_done[f], upto(s))
                v.tensor_scalar(p_one[:], p_exp[f][:], 1.0, None, ALU.add).then_inc(comb_step[f], 1)
                v.tensor_tensor(chosen[:], experts[:],
                                best_at[f][:, :, 0:TOPK].unsqueeze(3).to_broadcast(all_),
                                ALU.is_equal).then_inc(comb_step[f], 1)
                dve.wait_ge(comb_step[f], upto(s, 8, 0))
                v.reciprocal(score[:], p_one[:]).then_inc(comb_step[f], 1)
                dve.wait_ge(comb_step[f], upto(s, 8, 2))
                v.tensor_tensor(score_sum[:], score[:, :, 0], score[:, :, 1], ALU.add)\
                    .then_inc(comb_step[f], 1)
                dve.wait_ge(comb_step[f], upto(s, 8, 3))
                v.tensor_scalar(score_eps[:], score_sum[:], 1e-20, None, ALU.add)\
                    .then_inc(comb_step[f], 1)
                dve.wait_ge(comb_step[f], upto(s, 8, 4))
                v.reciprocal(score_inv[:], score_eps[:]).then_inc(comb_step[f], 1)
                dve.wait_ge(comb_step[f], upto(s, 8, 5))
                v.scalar_tensor_tensor(out=share[:], in0=score[:], scalar=ROUTE_SCALE,
                                       in1=score_inv[:].unsqueeze(2).to_broadcast([P, NT, TOPK]),
                                       op0=ALU.mult, op1=ALU.mult).then_inc(comb_step[f], 1)
                dve.wait_ge(comb_step[f], upto(s, 8, 6))
                v.tensor_tensor(chosen_w[:], chosen[:],
                                share[:].unsqueeze(3).to_broadcast(all_), ALU.mult)\
                    .then_inc(comb_step[f], 1)
                dve.wait_ge(comb_step[f], upto(s, 8, 7))
                v.tensor_tensor(comb[:], chosen_w[:, :, 0, :], chosen_w[:, :, 1, :], ALU.add)\
                    .then_inc(comb_done[f], 1)

            for e in range(NE):
                v.memset(experts[:, :, :, e], float(e))
            dve.wait_ge(consts, 2)
            walk(dve, tables["dve"], {
                "gated": gated, "weigh": weigh, "hidden_lo": hidden_lo, "residual": residual,
                "stats": stats, "norm": norm, "x_lo": x_lo, "shift_diff": shift_diff, "mix": mix,
                "mix_lo": mix_lo, "kv": kv, "scan": scan, "bonus": bonus, "receptance": receptance,
                "o_lo": o_lo, "out_residual": out_residual, "top2": top2, "combine": combine})


def kernel(**inputs):
    import numpy as np
    import concourse.bacc as bacc
    from concourse.bass_utils import run_bass_kernel_spmd

    a = {k: np.asarray(v) for k, v in inputs.items()}
    C = a["L0_attn_x"].shape[-1]
    KC = C // P

    def lhs(w):
        return w.T.reshape(KC, P, -1).transpose(1, 0, 2)

    chunks = []
    shared = a["L0_ffn_ws_gate"].shape[0] // P
    for c in range(shared):
        rows = slice(c * P, (c + 1) * P)
        chunks.append((a["L0_ffn_ws_gate"][rows], a["L0_ffn_ws_up"][rows],
                       a["L0_ffn_ws_down"][:, rows]))
    for e in range(a["L0_ffn_w_gate"].shape[0]):
        chunks.append((a["L0_ffn_w_gate"][e], a["L0_ffn_w_up"][e], a["L0_ffn_w_down"][e]))
    w_chunks = np.stack([
        np.concatenate([np.concatenate([lhs(g), lhs(u)], axis=2).reshape(P, -1), d.T], axis=1)
        for g, u, d in chunks])
    w_attn = np.stack([lhs(a[f"L0_attn_{n}"]) for n in ("Wk", "Wv", "Wr", "Wo")], axis=1)
    channels = np.stack([a[f"L0_attn_{n}"].reshape(KC, P).T for n in (
        "time_mix_k", "time_mix_v", "time_mix_r", "time_decay", "time_first", "ln_g", "ln_b")],
        axis=1)
    arrays = {"x": a["L0_attn_x"], "w_chunks": w_chunks, "w_attn": w_attn,
              "w_router": lhs(a["L0_ffn_gate_weight"]), "channels": channels}
    arrays = {f"in_{k}_dram": np.ascontiguousarray(v) for k, v in arrays.items()}

    nc = bacc.Bacc("TRN2", target_bir_lowering=False, num_devices=1)
    args = [nc.dram_tensor(k, v.shape, mybir.dt.from_np(v.dtype), kind="ExternalInput").ap()
            for k, v in arrays.items()]
    out = nc.dram_tensor("out_0_dram", a["L0_attn_x"].shape, F32, kind="ExternalOutput").ap()
    comb_dram = {f: nc.dram_tensor(f"comb{f}", [a["L0_ffn_w_gate"].shape[0], a["L0_attn_x"].shape[1]],
                                   F32).ap() for f in "AB"}
    program(nc, *args, comb_dram, out)
    r = run_bass_kernel_spmd(nc, [arrays], core_ids=[0])
    return r.results[0]["out_0_dram"]
```

```python
from contextlib import ExitStack

import concourse.bass as bass
from concourse import mybir

F32 = mybir.dt.float32
F16 = mybir.dt.float16
U32 = mybir.dt.uint32
ALU = mybir.AluOpType
ACT = mybir.ActivationFunctionType

P = 128
EPS = 1e-5
TOPK = 2
ROUTE_SCALE = 2.5
W_SCALE = 256.0
W_UNSCALE = 1.0 / W_SCALE
STEPS = 20
HALF = STEPS // 2


def upto(s, per=1, part=0):
    i, off = s
    return i * per + (off * per + part + 1)


def residuals(phase, s, n_seq):
    i, off = s
    if phase == "A":
        return 2 if isinstance(i, int) and i + off == 0 else i * 4 + off * 4
    return min(4 * (i + off) + 6, 4 * n_seq) if isinstance(i, int) else i * 4 + (off * 4 + 6)


def step_tables(n_chunks, n_shared):
    pe_mid = {0: [("r_proj", -1)], 2: [("scan_turn", -1)], 4: [("turn", -1, "o2")],
              7: [("turn", -1, "3")], 8: [("router", -1, "B")],
              10: [("router_turn", -1, "B"), ("turn", 1, "1")], 12: [("router", 1, "A")],
              16: [("router_turn", 1, "A")]}
    pe_post = {5: [("out_proj", -1)], 13: [("turn", 0, "2")], 17: [("kv_proj", 0, 0)],
               18: [("kv_proj", 0, 1)]}

    act_pre = {18: [("k_copy", 0, 0)], 19: [("k_copy", 0, 1)]}
    act_post = {0: [("r_copy", -1, 0), ("r_copy", -1, 1)],
                2: [("o_copy", -1, 0), ("o_copy", -1, 1)],
                4: [("o_affine", -1, 0), ("o_affine", -1, 1), ("o_hi", -1, 0), ("o_hi", -1, 1)],
                7: [("x_hi", -1, "3", 0), ("x_hi", -1, "3", 1)],
                10: [("router_turned", -1, "B"), ("x_hi", 1, "1", 0), ("x_hi", 1, "1", 1)],
                13: [("mix_in", 0, 0), ("mix_in", 0, 1)],
                15: [("mix_hi", 0, 0), ("mix_hi", 0, 1)],
                16: [("router_turned", 1, "A"), ("mix_hi", 0, 2), ("mix_hi", 0, 3)],
                18: [("mix_hi", 0, 4), ("mix_hi", 0, 5)]}

    dve_pre = {0: [("scan", -1, 1)], 1: [("receptance", -1)],
               3: [("stats", -1, "o")], 5: [("o_lo", -1, 0), ("o_lo", -1, 1)],
               6: [("out_residual", -1), ("stats", -1, "3")],
               8: [("x_lo", -1, "3", 0), ("x_lo", -1, "3", 1)],
               11: [("x_lo", 1, "1", 0), ("x_lo", 1, "1", 1)],
               12: [("stats", 0, "2")], 14: [("shift_diff", 0)],
               15: [("mix", 0, 0), ("mix", 0, 1)], 16: [("mix", 0, 2), ("mix", 0, 3)],
               17: [("mix_lo", 0, 2), ("mix_lo", 0, 3)],
               18: [("kv", 0, 0), ("mix", 0, 4), ("mix", 0, 5)],
               19: [("kv", 0, 1), ("mix_lo", 0, 4), ("mix_lo", 0, 5)]}
    dve_post = {0: [("bonus", -1, 0), ("bonus", -1, 1)], 1: [("residual", -2, "B")],
                3: [("norm", -1, "o")], 4: [("stats", 1, "1")], 6: [("norm", -1, "3")],
                7: [("norm", 1, "1")],
                8: [("top2", -1, "B")], 9: [("combine", -1, "B")], 11: [("residual", 0, "A")],
                12: [("norm", 0, "2"), ("top2", 1, "A")], 14: [("combine", 1, "A")],
                15: [("mix_lo", 0, 0), ("mix_lo", 0, 1)],
                19: [("scan", 0, 0)]}
    tables = {e: [] for e in ("pe", "act", "dve", "pool", "sp")}
    for k in range(STEPS):
        f, c = ("A", k) if k < HALF else ("B", k - HALF)
        seq = 0 if f == "A" else -1
        back = {n: (("A", k - n, 0) if k - n < HALF else ("B", k - n - HALF, -1)) if k >= n
                else ("B", HALF + k - n, -2) for n in (1, 2)}
        pe = [("gate_up", seq, f, c)]
        pe += pe_mid.get(k, []) + [("down", back[2][2], back[2][0], back[2][1])] + pe_post.get(k, [])
        tables["pe"].append(pe)
        last = (back[1][2], back[1][0], back[1][1])
        tables["act"].append([("hidden_hi", *last)] + act_pre.get(k, []) + [("silu", seq, f, c)]
                             + act_post.get(k, []))
        weigh = [("weigh", seq, f, c)] if c >= n_shared else []
        tables["dve"].append([("hidden_lo", *last)] + dve_pre.get(k, []) + [("gated", seq, f, c)]
                             + weigh + dve_post.get(k, []))
        tables["pool"].append({3: [("rstd", -1, "o")], 4: [("rstd", 1, "1")], 6: [("rstd", -1, "3")],
                               8: [("route_exp", -1, "B")], 12: [("rstd", 0, "2"),
                               ("route_exp", 1, "A")]}.get(k, []))
        tables["sp"].append({1: [("load_norm", 1), ("store", -2)], 10: [("spread", -1, "B")],
                             11: [("load", 1)], 16: [("spread", 1, "A")]}.get(k, []))
    return tables


def program(nc, x, w_chunks, w_attn, w_router, channels, comb_dram, out):
    NSEQ, T, C = x.shape
    NCH = w_chunks.shape[0]
    KC = C // P
    NT = T // P
    NE = w_router.shape[2]
    NSH = NCH - NE
    GU = 2 * KC * P
    assert NCH == HALF and T == 512 and C == 256
    MIX_K, MIX_V, MIX_R, DECAY, FIRST, LN_G, LN_B = range(7)

    WAHEAD = 3
    HBUF = 5
    assert NCH % HBUF == 0 and NCH % 2 == 0
    PHASE = {"1": "A", "3": "B"}
    tables = step_tables(NCH, NSH)
    KINDS = {"gate_up": "products", "silu": "values", "gated": "values", "weigh": "values",
             "hidden_hi": "hidden", "hidden_lo": "hidden", "down": "down",
             "residual": "residual"}
    START, STOP, LAST = 1, NSEQ - 2, NSEQ - 1
    G, V = "G", "V"
    BESIDE_FIRST = (G, 12, V, G, 13, range(14, 16), V, G, range(16, STEPS), G, 14, 15, 16, V, 17, V,
                    18, G, 19, 0, 1, V, 2, G, 3, V, 4, G, 5, V, G, 6, V, 7, G, 8, V, G, 9, V)
    BESIDE_LAST = (G, 10, 12, V, G, 13, 14, 15, V, G, G, 16, 17, V, V, 18, G, 19, 0, 1, V, 2, G, 3,
                   V, G, 4, V, G, 5, V, G, 6, V, G, 7, V)

    def kind(what, off):
        return KINDS.get(what, "prep" if off == 1 else "chain")

    FFN = ("products", "values", "hidden", "down")
    REST = ("residual", "prep", "chain")
    ALL = FFN + REST

    def beside(iteration, first, chain_of, pattern, kinds_of):
        order, opened, closed = [], 0, 0
        for what in pattern:
            if what == G:
                order.append((iteration, first + opened, ("products",)))
                opened += 1
            elif what == V:
                order.append((iteration, first + closed, ("values", "hidden", "down")[:closed + 1]))
                closed += 1
            elif isinstance(what, range):
                order += [(chain_of, k, ("prep",)) for k in what]
            else:
                order.append((chain_of + (what < HALF), what, kinds_of(what)))
        assert opened == closed == NCH
        return order

    prologue = [(-1, k, ALL) for k in range(13)] + [(0, 0, ALL)]
    prologue += [(-1, k, ALL) for k in range(13, 16)] + [(0, 1, ALL)]
    prologue += [(-1, k, ALL) for k in range(16, STEPS)] + [(0, k, ALL) for k in range(2, HALF)]
    prologue += [(0, 10, ("prep",)), (0, 10, ("hidden", "down")),
                 (0, 11, ("prep", "down", "residual"))]
    prologue += beside(1, 0, 0, BESIDE_FIRST, lambda k: REST if k < 14 else ("chain",))
    epilogue = [(STOP, k, ALL) for k in range(HALF, STEPS)] + [(LAST, k, ALL) for k in range(HALF)]
    epilogue += [(LAST, 10, ("hidden", "down")), (LAST, 11, ("down", "residual"))]
    epilogue += beside(LAST, HALF, LAST, BESIDE_LAST, lambda k: ("prep", "chain"))
    epilogue += [(LAST + 1, 0, ("hidden", "down")), (LAST + 1, 10, ("products",)),
                 (LAST + 1, 8, REST), (LAST + 1, 1, ("down", "residual")),
                 (LAST + 1, 11, ("products",)), (LAST + 1, 9, REST),
                 (LAST + 1, 10, ("values",) + REST), (LAST + 1, 11, ALL[1:])]
    epilogue += [(LAST + 1, k, ALL) for k in range(12, STEPS)]
    epilogue += [(LAST + 2, k, ALL) for k in range(2)]
    loop = [(0, k) for k in range(HALF, STEPS)] + [(1, k) for k in range(HALF)]

    def live(i, off):
        return not isinstance(i, int) or 0 <= i + off < NSEQ

    def walk(eng, table, do):
        def steps(some):
            for i, k, kinds in some:
                for what, off, *args in table[k]:
                    if live(i, off) and kind(what, off) in kinds:
                        do[what]((i, off), *args)
        steps(prologue)
        with eng.Fori(START, STOP) as i:
            for later, k in loop:
                for what, off, *args in table[k]:
                    do[what]((i, off + later), *args)
        steps(epilogue)

    def whole_stream(table):
        inside = [(i + later, k, ALL) for i in range(START, STOP) for later, k in loop]
        for steps, in_loop in ((prologue, False), (inside, True), (epilogue, False)):
            for i, k, kinds in steps:
                for what, off, *args in table[k]:
                    if live(i, off) and kind(what, off) in kinds:
                        yield what, i + off, args, in_loop

    OUT_BANK, RING = 0, (2, 3, 4, 5, 6, 7)
    USES = {"gate_up": 2, "turn": 2, "scan_turn": 2, "out_proj": 2, "kv_proj": 2, "r_proj": 2,
            "router": 1, "router_turn": 1}
    PASSED = {"router_turn": 2}
    banks, before, held = {}, {}, {}
    n_ring = 0
    for what, seq, args, in_loop in whole_stream(tables["pe"]):
        for b in range(USES.get(what, 0)):
            bank = RING[n_ring % len(RING)]
            n_ring += 1
            banks[what, *args, b, seq] = bank
            if bank in held:
                t, s = held[bank]
                before[what, *args, b, seq] = (t, s - seq)
            held[bank] = ((what, *args, b), seq)
        if in_loop:
            n_ring += PASSED.get(what, 0)
    IN_LOOP = NSEQ // 2
    for later, k in loop:
        for what, off, *args in tables["pe"][k]:
            for b in range(USES.get(what, 0)):
                seqs = range(START + later + off, STOP + later + off)
                assert len({before[what, *args, b, seq] for seq in seqs}) == 1
    assert all(banks[t] == banks[*t[:-1], IN_LOOP + 1] and before[t] == before[*t[:-1], IN_LOOP + 1]
               for t in banks if t[-1] == IN_LOOP)

    def at(s):
        i, off = s
        return i + off if isinstance(i, int) else IN_LOOP

    def bank_of(s, *task_b):
        return banks[*task_b, at(s)]

    with ExitStack() as ctx:
        def sb(name, shape, dt=F32):
            return ctx.enter_context(nc.sbuf_tensor(name, shape, dt))

        def sem(name):
            return ctx.enter_context(nc.semaphore(name))

        ps = ctx.enter_context(nc.psum_tensor("ps", [P, 8, 512], F32))

        w_hi = sb("w_hi", [P, NCH, GU + C], F16)
        w_lo = sb("w_lo", [P, NCH, GU + C], F16)
        a_hi = sb("a_hi", [P, 4, KC, C], F16)
        a_lo = sb("a_lo", [P, 4, KC, C], F16)
        r_both = sb("r_both", [P, KC, 2, NE], F16)
        r_stage = sb("r_stage", [P, KC, NE])
        chan = sb("chan", [P, 7, KC])
        decay = sb("decay", [P, KC])
        arena = sb("arena", [P, NCH * (GU + C) + 4 * KC * C])
        w_stage = arena[:, 0:NCH * (GU + C)].rearrange("p (c n) -> p c n", c=NCH)
        a_stage = arena[:, NCH * (GU + C):].rearrange("p (a k n) -> p a k n", a=4, k=KC)
        mix32 = arena[:, 0:6 * T].rearrange("p (j t) -> p j t", j=6)

        def tile_at(n):
            return arena[:, (6 + 2 * n) * T:(8 + 2 * n) * T].rearrange("p (m t) -> p m t", m=KC)

        diff, k_sb, kv_sb, state, r_sb, o_aff = (tile_at(n) for n in range(6))

        ident = sb("ident", [P, P])
        experts = sb("experts", [P, NT, TOPK, NE])
        neg_half = sb("neg_half", [P, NT])
        inv_e = sb("inv_e", [P, NT, TOPK])
        euler = sb("euler", [P, KC])
        eps_t = sb("eps_t", [P, NT])

        x0 = sb("x0", [P, NT, C])
        x_norm = sb("x_norm", [P, NT, C])
        x1 = sb("x1", [P, NT, C])
        x2 = sb("x2", [P, NT, C])
        x3 = sb("x3", [P, NT, C])
        o_tok = sb("o_tok", [P, NT, C])
        LNS = ("1", "2", "o", "3")
        normed = {n: sb(f"normed{n}", [P, NT, C]) for n in ("1", "2", "3")} | {"o": o_tok}
        ln_in = {"1": x_norm, "2": x1, "o": o_tok}
        stat = {n: sb(f"stat{n}", [P, NT, 6]) for n in LNS}
        mean_var = {n: sb(f"mean_var{n}", [P, NT, 2]) for n in LNS}
        var_eps = {n: sb(f"var_eps{n}", [P, NT]) for n in LNS}
        rstd_t = {n: sb(f"rstd{n}", [P, NT]) for n in LNS}

        xh = {f: sb(f"xh{f}", [P, KC, T], F16) for f in "AB"}
        xl = {f: sb(f"xl{f}", [P, KC, T], F16) for f in "AB"}
        shifted = sb("shifted", [P, KC, T + 1])
        mix_h = sb("mix_h", [P, 6, T], F16)
        mix_l = sb("mix_l", [P, 6, T], F16)
        oh = sb("oh", [P, KC, T], F16)
        ol = sb("ol", [P, KC, T], F16)

        silu_t = sb("silu_t", [P, 2, T])
        gated_t = sb("gated_t", [P, 2, T])
        hid = sb("hid", [P, 2, T])
        hid_h = sb("hid_h", [P, HBUF, T], F16)
        hid_l = sb("hid_l", [P, HBUF, T], F16)

        logits_lo = sb("logits_lo", [P, NT, NE])
        logits = {f: sb(f"logits{f}", [P, NT, NE]) for f in "AB"}
        best = {f: sb(f"best{f}", [P, NT, NE]) for f in "AB"}
        best_at = {f: sb(f"best_at{f}", [P, NT, NE], U32) for f in "AB"}
        p_exp = {f: sb(f"p_exp{f}", [P, NT, TOPK]) for f in "AB"}
        p_one = sb("p_one", [P, NT, TOPK])
        score = sb("score", [P, NT, TOPK])
        score_sum = sb("score_sum", [P, NT])
        score_eps = sb("score_eps", [P, NT])
        score_inv = sb("score_inv", [P, NT])
        share = sb("share", [P, NT, TOPK])
        chosen = sb("chosen", [P, NT, TOPK, NE])
        chosen_w = sb("chosen_w", [P, NT, TOPK, NE])
        comb = sb("comb", [P, NT, NE])
        comb_t = {f: sb(f"comb_t{f}", [NE, T]) for f in "AB"}
        AT_ONCE = 2
        spread_t = {f: sb(f"spread_t{f}", [P, NE, T]) for f in "AB"}

        w_in = [sem(f"w_in{c}") for c in range(NCH)]
        attn_in, router_in, chan_in = sem("attn_in"), sem("router_in"), sem("chan_in")
        x_in, x_norm_in, stored = sem("x_in"), sem("x_norm_in"), sem("stored")
        w_hi_done, w_split = sem("w_hi_done"), sem("w_split")
        const_set, consts = sem("const_set"), sem("consts")
        gate_done = {f: sem(f"gate_done{f}") for f in "AB"}
        up_done = {f: sem(f"up_done{f}") for f in "AB"}
        down_done = {f: sem(f"down_done{f}") for f in "AB"}
        comb_out = {f: sem(f"comb_out{f}") for f in "AB"}
        spread_in = {f: [sem(f"spread_in{f}{q}") for q in range(NE // AT_ONCE)] for f in "AB"}
        silu_done = {f: sem(f"silu_done{f}") for f in "AB"}
        gated_done = {f: sem(f"gated_done{f}") for f in "AB"}
        weigh_done = {f: sem(f"weigh_done{f}") for f in "AB"}
        hi_done = {f: sem(f"hi_done{f}") for f in "AB"}
        lo_done = {f: sem(f"lo_done{f}") for f in "AB"}
        residual_done, x2_done = sem("residual_done"), sem("x2_done")
        stats_done = {n: sem(f"stats_done{n}") for n in LNS}
        moments_done = {n: sem(f"moments_done{n}") for n in LNS}
        var_done = {n: sem(f"var_done{n}") for n in LNS}
        rstd_done = {n: sem(f"rstd_done{n}") for n in LNS}
        norm_done = {n: sem(f"norm_done{n}") for n in LNS}
        turned = {n: sem(f"turned{n}") for n in ("1", "2", "o2", "3")}
        turned_hi = {n: sem(f"turned_hi{n}") for n in ("1", "3")}
        turned_lo = {n: sem(f"turned_lo{n}") for n in ("1", "3")}
        mix_in_done, diff_done = sem("mix_in_done"), sem("diff_done")
        mix_done, mix_hi_done, mix_lo_done = sem("mix_done"), sem("mix_hi_done"), sem("mix_lo_done")
        k_done, v_done, r_done = sem("k_done"), sem("v_done"), sem("r_done")
        k_copied, r_copied = sem("k_copied"), sem("r_copied")
        kv_done, scan_done, bonus_done = sem("kv_done"), sem("scan_done"), sem("bonus_done")
        mixed_done, scan_turned, o_copied = sem("mixed_done"), sem("scan_turned"), sem("o_copied")
        o_affine_done = sem("o_affine_done")
        o_hi_done, o_lo_done = sem("o_hi_done"), sem("o_lo_done")
        out_proj_done = sem("out_proj_done")
        router_done = {f: sem(f"router_done{f}") for f in "AB"}
        logits_lo_out = {f: sem(f"logits_lo_out{f}") for f in "AB"}
        logits_out = {f: sem(f"logits_out{f}") for f in "AB"}
        max_done = {f: sem(f"max_done{f}") for f in "AB"}
        top2_done = {f: sem(f"top2_done{f}") for f in "AB"}
        exp_done = {f: sem(f"exp_done{f}") for f in "AB"}
        comb_step = {f: sem(f"comb_step{f}") for f in "AB"}
        comb_done = {f: sem(f"comb_done{f}") for f in "AB"}
        comb_turned = {f: sem(f"comb_turned{f}") for f in "AB"}
        comb_copied = {f: sem(f"comb_copied{f}") for f in "AB"}

        def x2_of(s):
            return x_norm if at(s) == LAST else x2

        def own_wait(eng, signal, value):
            eng.wait_ge(consts, 2)
            eng.wait_ge(signal, value)

        def silu_before(s, f, c):
            i, off = s
            if c >= 2:
                return s, f, c - 2
            prev, other = ((i, off - 2), "B") if f == "A" else ((i, off + 1), "A")
            if live(i, prev[1]):
                return prev, other, c + NCH - 2
            return ((i, off - 1), f, c + NCH - 2) if live(i, off - 1) else (None, f, c)

        def released(task, s):
            what, *args, b = task
            if what == "gate_up":
                f, c = args
                return (silu_done, gated_done)[b][f], upto(s, NCH, c)
            if what == "turn":
                n = args[0]
                if n == "2":
                    return mix_in_done, upto(s, KC, b)
                if n == "o2":
                    return o_affine_done, upto(s, KC, b)
                return turned_lo[n], upto(s, KC, b)
            if what == "scan_turn":
                return o_copied, upto(s, 2, b)
            if what == "out_proj":
                return x2_done, upto(s, 2, b)
            if what == "kv_proj":
                return (k_copied, kv_done)[b], upto(s, KC, args[0])
            if what == "r_proj":
                return r_copied, upto(s, KC, b)
            if what == "router":
                return logits_out[args[0]], upto(s)
            return comb_copied[args[0]], upto(s)

        block = ctx.enter_context(nc.Block())

        @block.sync
        def _(sp):
            x_tok = x.rearrange("s (j p) c -> s p j c", p=P)
            out_tok = out.rearrange("s (j p) c -> s p j c", p=P)

            def load_next(s):
                i, off = s
                if isinstance(i, int) and i + off == 0:
                    return
                sp.wait_ge(residual_done, residuals("A", (i, off - 1), NSEQ))
                sp.dma_start(x0[:], x_tok[i + off]).then_inc(x_in, 16)

            def store(s):
                i, off = s
                sp.wait_ge(residual_done, residuals("B", s, NSEQ))
                sp.dma_start(out_tok[i + off], x3[:]).then_inc(stored, 16)

            def load_norm(s):
                i, off = s
                if isinstance(i, int) and i + off == 0:
                    return
                sp.wait_ge(norm_done["1"], i + off)
                sp.dma_start(x_norm[:], x_tok[i + off]).then_inc(x_norm_in, 16)

            def spread(s, f):
                sp.wait_ge(comb_copied[f], upto(s))
                sp.dma_start(comb_dram[f], comb_t[f][:]).then_inc(comb_out[f], 16)
                sp.wait_ge(comb_out[f], upto(s, 16, 15))
                for q in range(NE // AT_ONCE):
                    some = slice(q * AT_ONCE, (q + 1) * AT_ONCE)
                    sp.dma_start(spread_t[f][:, some, :],
                                 comb_dram[f][some, :].partition_broadcast(P))\
                        .then_inc(spread_in[f][q], 16)

            sp.dma_start(x_norm[:], x_tok[0]).then_inc(x_norm_in, 16)
            sp.dma_start(r_stage[:], w_router).then_inc(router_in, 16)
            for c in range(0, NCH):
                sp.dma_start(w_stage[:, c, :], w_chunks[c]).then_inc(w_in[c], 16)
            sp.dma_start(x0[:], x_tok[0]).then_inc(x_in, 16)
            sp.dma_start(a_stage, w_attn).then_inc(attn_in, 16)
            walk(sp, tables["sp"], {"load": load_next, "load_norm": load_norm, "store": store,
                                    "spread": spread})
            sp.wait_ge(stored, 16 * (NSEQ + 1))

        @block.gpsimd
        def _(pool):
            g = nc.gpsimd
            g.memset(ident[:], 0.0).then_inc(const_set, 1)
            g.memset(neg_half[:], -0.5).then_inc(const_set, 1)
            g.memset(inv_e[:], 0.36787944117144233).then_inc(const_set, 1)
            g.memset(euler[:], 2.718281828459045).then_inc(const_set, 1)
            g.memset(shifted[:, :, 0:1], 0.0).then_inc(const_set, 1)
            g.memset(eps_t[:], EPS).then_inc(const_set, 1)
            pool.wait_ge(const_set, 6)
            g.affine_select(out=ident[:], in_=ident[:], compare_op=ALU.not_equal, fill=1.0, base=0,
                            pattern=[[-1, P]], channel_multiplier=1).then_inc(consts, 1)
            pool.wait_ge(chan_in, 16)
            g.tensor_tensor(decay[:], euler[:], chan[:, DECAY, :], ALU.pow).then_inc(consts, 1)

            def rstd(s, n):
                pool.wait_ge(moments_done[n], upto(s))
                g.tensor_tensor(var_eps[n][:], mean_var[n][:, :, 1], eps_t[:], ALU.add)\
                    .then_inc(var_done[n], 1)
                pool.wait_ge(var_done[n], upto(s))
                g.tensor_tensor(rstd_t[n][:], var_eps[n][:], neg_half[:], ALU.pow)\
                    .then_inc(rstd_done[n], 1)

            def route_exp(s, f):
                pool.wait_ge(top2_done[f], upto(s))
                g.tensor_tensor(p_exp[f][:], inv_e[:], best[f][:, :, 0:TOPK], ALU.pow)\
                    .then_inc(exp_done[f], 1)

            walk(pool, tables["pool"], {"rstd": rstd, "route_exp": route_exp})

        @block.tensor
        def _(pe):
            def bank_free(s, *task_b):
                if (*task_b, at(s)) in before:
                    task, rel = before[(*task_b, at(s))]
                    pe.wait_ge(*released(task, (s[0], s[1] + rel)))
                return bank_of(s, *task_b)

            def three(out_ap, hi_w, lo_w, hi_x, lo_x, first, last, hi_there=None, lo_there=None):
                if hi_there:
                    pe.wait_ge(*hi_there)
                nc.tensor.matmul(out_ap, hi_w, hi_x, start=first, stop=False)
                nc.tensor.matmul(out_ap, lo_w, hi_x, start=False, stop=False)
                if lo_there:
                    pe.wait_ge(*lo_there)
                return nc.tensor.matmul(out_ap, hi_w, lo_x, start=False, stop=last)

            def gate_up(s, f, c):
                i, off = s
                n = "1" if f == "A" else "3"
                if f == "A" and isinstance(i, int) and i + off == 0:
                    pe.wait_ge(w_split, c + 2)
                for b, done in ((0, gate_done), (1, up_done)):
                    bank = bank_free(s, "gate_up", f, c, b)
                    for k in range(KC):
                        cols = slice(k * 2 * P + b * P, k * 2 * P + (b + 1) * P)
                        x_there = ((turned_hi[n], upto(s, KC, k)), (turned_lo[n], upto(s, KC, k))) \
                            if c == 0 and b == 0 else ()
                        mm = three(ps[:, bank, :], w_hi[:, c, cols], w_lo[:, c, cols],
                                   xh[f][:, k, :], xl[f][:, k, :], k == 0, k == KC - 1, *x_there)
                    mm.then_inc(done[f], 1)

            def down(s, f, c):
                i, off = s
                pe.wait_ge(lo_done[f], upto(s, NCH, c))
                if c == 0 and not (f == "A" and isinstance(i, int) and i + off == 0):
                    if f == "A":
                        pe.wait_ge(residual_done, i * 4 + (off * 4 - 2))
                    else:
                        v = i * 4 + (off * 4 + 4)
                        pe.wait_ge(residual_done, min(v, 4 * NSEQ - 2) if isinstance(i, int) else v)
                b = c % HBUF
                for j in range(NT):
                    tok = slice(j * P, (j + 1) * P)
                    half = ps[:, OUT_BANK + j // 2, (j % 2) * C:(j % 2 + 1) * C]
                    wh, wl = w_hi[:, c, GU:], w_lo[:, c, GU:]
                    nc.tensor.matmul(half, hid_h[:, b, tok], wh, start=(c == 0 and j % 2 == 0),
                                     stop=False, skip_group_check=True)
                    nc.tensor.matmul(half, hid_h[:, b, tok], wl, start=False, stop=False,
                                     skip_group_check=True)
                    mm = nc.tensor.matmul(half, hid_l[:, b, tok], wh, start=False,
                                          stop=(c == NCH - 1 and j % 2 == 1), skip_group_check=True)
                mm.then_inc(down_done[f], 1)

            def turn(s, n):
                pe.wait_ge(norm_done[n[0]], upto(s))
                for m in range(KC):
                    bank = bank_free(s, "turn", n, m)
                    for j in range(NT):
                        mm = nc.tensor.transpose(ps[:, bank, j * P:(j + 1) * P],
                                                 normed[n[0]][:, j, m * P:(m + 1) * P], ident[:])
                    mm.then_inc(turned[n], 1)

            def kv_proj(s, m):
                if m == 0 and at(s) == 0:
                    pe.wait_ge(w_split, NCH + 2)
                for b, done in ((0, k_done), (1, v_done)):
                    bank = bank_free(s, "kv_proj", m, b)
                    project(s, bank, b, m).then_inc(done, 1)

            def project(s, bank, which, m):
                for k in range(KC):
                    cols, j = slice(m * P, (m + 1) * P), which * KC + k
                    if m == 0:
                        pe.wait_ge(mix_lo_done, upto(s, 6, j))
                    mm = three(ps[:, bank, :], a_hi[:, which, k, cols], a_lo[:, which, k, cols],
                               mix_h[:, j, :], mix_l[:, j, :], k == 0, k == KC - 1)
                return mm

            def r_proj(s):
                for m in range(KC):
                    bank = bank_free(s, "r_proj", m)
                    project(s, bank, 2, m).then_inc(r_done, 1)

            def scan_turn(s):
                pe.wait_ge(mixed_done, upto(s))
                for b in range(2):
                    bank = bank_free(s, "scan_turn", b)
                    for j in range(2):
                        for m in range(KC):
                            t0 = (2 * b + j) * P
                            mm = nc.tensor.transpose(ps[:, bank, j * C + m * P:j * C + (m + 1) * P],
                                                     state[:, m, t0:t0 + P], ident[:])
                    mm.then_inc(scan_turned, 1)

            def out_proj(s):
                bank = [bank_free(s, "out_proj", b) for b in range(2)]
                for k in range(KC):
                    pe.wait_ge(o_lo_done, upto(s, KC, k))
                    for b in range(2):
                        for j in range(2):
                            tok = slice((2 * b + j) * P, (2 * b + j + 1) * P)
                            half = ps[:, bank[b], j * C:(j + 1) * C]
                            nc.tensor.matmul(half, oh[:, k, tok], a_hi[:, 3, k, :],
                                             start=(k == 0 and j == 0), stop=False,
                                             skip_group_check=True)
                            nc.tensor.matmul(half, oh[:, k, tok], a_lo[:, 3, k, :], start=False,
                                             stop=False, skip_group_check=True)
                            mm = nc.tensor.matmul(half, ol[:, k, tok], a_hi[:, 3, k, :], start=False,
                                                  stop=(k == KC - 1 and j == 1),
                                                  skip_group_check=True)
                        if k == KC - 1:
                            mm.then_inc(out_proj_done, 1)

            def router(s, f):
                pe.wait_ge(turned_lo["1" if f == "A" else "3"], upto(s, KC, KC - 1))
                if f == "A" and at(s) == 0:
                    pe.wait_ge(w_split, 1)
                bank = bank_free(s, "router", f, 0)
                for j in range(NT):
                    tok = slice(j * P, (j + 1) * P)
                    cell = ps[:, bank, j * 2 * NE:(j + 1) * 2 * NE]
                    for k in range(KC):
                        nc.tensor.matmul(cell, xh[f][:, k, tok],
                                         r_both[:, k, :, :].rearrange("p h e -> p (h e)"),
                                         start=(j == 0 and k == 0), stop=False,
                                         skip_group_check=True)
                        mm = nc.tensor.matmul(cell[:, 0:NE], xl[f][:, k, tok], r_both[:, k, 0, :],
                                              start=False, stop=(j == NT - 1 and k == KC - 1),
                                              skip_group_check=True)
                mm.then_inc(router_done[f], 1)

            def router_turn(s, f):
                pe.wait_ge(comb_done[f], upto(s))
                bank = bank_free(s, "router_turn", f, 0)
                for j in range(NT):
                    mm = nc.tensor.transpose(ps[0:NE, bank, j * P:(j + 1) * P], comb[:, j, :],
                                             ident[:])
                mm.then_inc(comb_turned[f], 1)

            pe.wait_ge(consts, 1)
            walk(pe, tables["pe"], {
                "gate_up": gate_up, "down": down, "turn": turn,
                "kv_proj": kv_proj, "r_proj": r_proj, "scan_turn": scan_turn, "out_proj": out_proj,
                "router": router, "router_turn": router_turn})

        @block.scalar
        def _(act):
            act.dma_start(chan[:], channels).then_inc(chan_in, 16)

            def split_weights(c):
                if c < 0:
                    act.wait_ge(router_in, 16)
                    nc.scalar.activation(r_both[:, :, 0, :], r_stage[:], ACT.Copy, scale=W_SCALE)\
                        .then_inc(w_hi_done, 1)
                elif c < NCH:
                    act.wait_ge(w_in[c], 16)
                    nc.scalar.activation(w_hi[:, c, :], w_stage[:, c, :], ACT.Copy, scale=W_SCALE)\
                        .then_inc(w_hi_done, 1)
                else:
                    act.wait_ge(attn_in, 16)
                    nc.scalar.activation(a_hi[:], a_stage, ACT.Copy, scale=W_SCALE)\
                        .then_inc(w_hi_done, 1)

            def silu(s, f, c):
                if f == "A" and isinstance(s[0], int) and sum(s) == 0:
                    if c + WAHEAD <= NCH:
                        split_weights(c + WAHEAD)
                act.wait_ge(gate_done[f], upto(s, NCH, c))
                last, lf, lc = silu_before(s, f, c)
                if last is not None:
                    act.wait_ge(gated_done[lf], upto(last, NCH, lc))
                nc.scalar.activation(silu_t[:, c % 2, :], ps[:, bank_of(s, "gate_up", f, c, 0), :],
                                     ACT.Silu, scale=W_UNSCALE).then_inc(silu_done[f], 1)

            def hidden_hi(s, f, c):
                if c < NSH:
                    act.wait_ge(gated_done[f], upto(s, NCH, c))
                else:
                    act.wait_ge(weigh_done[f], upto(s, NE, c - NSH))
                b = c % HBUF
                nc.scalar.copy(hid_h[:, b, :], hid[:, c % 2, :]).then_inc(hi_done[f], 1)

            def x_hi(s, n, m):
                act.wait_ge(turned[n], upto(s, KC, m))
                nc.scalar.copy(xh[PHASE[n]][:, m, :], ps[:, bank_of(s, "turn", n, m), :])\
                    .then_inc(turned_hi[n], 1)

            def mix_in(s, m):
                act.wait_ge(turned["2"], upto(s, KC, m))
                nc.scalar.copy(shifted[:, m, 1:T + 1], ps[:, bank_of(s, "turn", "2", m), :])\
                    .then_inc(mix_in_done, 1)

            def mix_hi(s, j):
                act.wait_ge(mix_done, upto(s, 6, j))
                nc.scalar.copy(mix_h[:, j, :], mix32[:, j, :]).then_inc(mix_hi_done, 1)

            def k_copy(s, m):
                act.wait_ge(k_done, upto(s, KC, m))
                nc.scalar.activation(k_sb[:, m, :], ps[:, bank_of(s, "kv_proj", m, 0), :], ACT.Copy,
                                     scale=W_UNSCALE).then_inc(k_copied, 1)

            def r_copy(s, m):
                act.wait_ge(r_done, upto(s, KC, m))
                nc.scalar.activation(r_sb[:, m, :], ps[:, bank_of(s, "r_proj", m), :], ACT.Copy,
                                     scale=W_UNSCALE).then_inc(r_copied, 1)

            def o_copy(s, b):
                act.wait_ge(scan_turned, upto(s, 2, b))
                nc.scalar.copy(o_tok[:, 2 * b:2 * b + 2, :],
                               ps[:, bank_of(s, "scan_turn", b), :]
                               .rearrange("p (j c) -> p j c", j=2)).then_inc(o_copied, 1)

            def o_affine(s, m):
                act.wait_ge(turned["o2"], upto(s, KC, m))
                nc.scalar.activation(o_aff[:, m, :], ps[:, bank_of(s, "turn", "o2", m), :],
                                     ACT.Identity, bias=chan[:, LN_B, m:m + 1],
                                     scale=chan[:, LN_G, m:m + 1])\
                    .then_inc(o_affine_done, 1)

            def o_hi(s, m):
                act.wait_ge(o_affine_done, upto(s, KC, m))
                nc.scalar.copy(oh[:, m, :], o_aff[:, m, :]).then_inc(o_hi_done, 1)

            def router_turned(s, f):
                act.wait_ge(comb_turned[f], upto(s))
                nc.scalar.copy(comb_t[f][:], ps[0:NE, bank_of(s, "router_turn", f, 0), :])\
                    .then_inc(comb_copied[f], 1)

            act.wait_ge(consts, 1)
            nc.scalar.activation(silu_t[:, 1, 0:1], ident[:, 0:1], ACT.Silu)
            for c in range(-1, WAHEAD):
                split_weights(c)
            act.wait_ge(chan_in, 16)
            walk(act, tables["act"], {
                "silu": silu, "hidden_hi": hidden_hi, "x_hi": x_hi, "mix_in": mix_in,
                "mix_hi": mix_hi, "k_copy": k_copy, "r_copy": r_copy, "o_copy": o_copy,
                "o_affine": o_affine, "o_hi": o_hi, "router_turned": router_turned})

        @block.vector
        def _(dve):
            v = nc.vector

            def split_weights(c):
                dve.wait_ge(w_hi_done, c + 2)
                if c < 0:
                    hi, lo, full = r_both[:, :, 0, :], r_both[:, :, 1, :], r_stage[:]
                elif c < NCH:
                    hi, lo, full = w_hi[:, c, :], w_lo[:, c, :], w_stage[:, c, :]
                else:
                    flat = "p a k n -> p (a k n)"
                    hi, lo, full = (a_hi[:].rearrange(flat), a_lo[:].rearrange(flat),
                                    a_stage.rearrange(flat))
                v.scalar_tensor_tensor(out=lo, in0=full, scalar=W_SCALE, in1=hi, op0=ALU.mult,
                                       op1=ALU.subtract).then_inc(w_split, 1)

            def gated(s, f, c):
                if f == "A" and isinstance(s[0], int) and sum(s) == 0:
                    if c + WAHEAD <= NCH:
                        split_weights(c + WAHEAD)
                dve.wait_ge(silu_done[f], upto(s, NCH, c))
                dve.wait_ge(up_done[f], upto(s, NCH, c))
                to = hid if c < NSH else gated_t
                v.scalar_tensor_tensor(out=to[:, c % 2, :],
                                       in0=ps[:, bank_of(s, "gate_up", f, c, 1), :],
                                       scalar=W_UNSCALE, in1=silu_t[:, c % 2, :], op0=ALU.mult,
                                       op1=ALU.mult).then_inc(gated_done[f], 1)

            def weigh(s, f, c):
                dve.wait_ge(gated_done[f], upto(s, NCH, c))
                dve.wait_ge(spread_in[f][(c - NSH) // AT_ONCE], upto(s, 16, 15))
                v.tensor_tensor(hid[:, c % 2, :], gated_t[:, c % 2, :],
                                spread_t[f][:, c - NSH, :], ALU.mult)\
                    .then_inc(weigh_done[f], 1)

            def hidden_lo(s, f, c):
                dve.wait_ge(hi_done[f], upto(s, NCH, c))
                b = c % HBUF
                v.tensor_tensor(hid_l[:, b, :], hid[:, c % 2, :], hid_h[:, b, :], ALU.subtract)\
                    .then_inc(lo_done[f], 1)

            def residual(s, f):
                i, off = s
                dve.wait_ge(down_done[f], upto(s, NCH, NCH - 1))
                if f == "A":
                    dve.wait_ge(x_in, upto(s, 16, 15))
                else:
                    dve.wait_ge(x2_done, upto(s, 2, 1))
                    dve.wait_ge(stored, upto(s, 16, 15))
                src, dst = (x0, x1) if f == "A" else (x2_of(s), x3)
                for b in range(2):
                    v.scalar_tensor_tensor(
                        out=dst[:, 2 * b:2 * b + 2, :].rearrange("p j c -> p (j c)"),
                        in0=ps[:, OUT_BANK + b, :], scalar=0.5 * W_UNSCALE,
                        in1=src[:, 2 * b:2 * b + 2, :].rearrange("p j c -> p (j c)"),
                        op0=ALU.mult, op1=ALU.add).then_inc(residual_done, 1)

            def stats(s, n):
                of_all = upto(s) if isinstance(s[0], int) else dve.to_reg(upto(s))
                if n == "1":
                    dve.wait_ge(x_norm_in, upto(s, 16, 15))
                elif n == "2":
                    dve.wait_ge(residual_done, residuals("A", s, NSEQ))
                elif n == "o":
                    dve.wait_ge(o_copied, upto(s, 2, 1))
                else:
                    dve.wait_ge(x2_done, upto(s, 2, 1))
                x_in_ln = x2_of(s) if n == "3" else ln_in[n]
                for j in range(NT):
                    ins = v.bn_stats(out=stat[n][:, j, :], in_=x_in_ln[:, j, :])
                ins.then_inc(stats_done[n], 1)
                own_wait(dve, stats_done[n], of_all)
                for j in range(NT):
                    ins = v.bn_aggr(out=mean_var[n][:, j, :], in_=stat[n][:, j, :])
                ins.then_inc(moments_done[n], 1)

            def norm(s, n):
                if n == "1" and at(s) == 0:
                    for c in range(-1, 1):
                        split_weights(c)
                dve.wait_ge(moments_done[n], upto(s))
                dve.wait_ge(rstd_done[n], upto(s))
                x_in_ln = x2_of(s) if n == "3" else ln_in[n]
                for j in range(NT):
                    ins = v.tensor_scalar(normed[n][:, j, :], x_in_ln[:, j, :],
                                          mean_var[n][:, j, 0:1], rstd_t[n][:, j:j + 1],
                                          ALU.subtract, ALU.mult)
                ins.then_inc(norm_done[n], 1)
                if n == "1" and at(s) == 0:
                    for c in range(1, WAHEAD):
                        split_weights(c)

            def x_lo(s, n, m):
                dve.wait_ge(turned_hi[n], upto(s, KC, m))
                v.tensor_tensor(xl[PHASE[n]][:, m, :], ps[:, bank_of(s, "turn", n, m), :],
                                xh[PHASE[n]][:, m, :], ALU.subtract).then_inc(turned_lo[n], 1)

            def shift_diff(s):
                dve.wait_ge(mix_in_done, upto(s, KC, KC - 1))
                v.tensor_tensor(diff, shifted[:, :, 1:T + 1], shifted[:, :, 0:T], ALU.subtract)\
                    .then_inc(diff_done, 1)

            def mix(s, j):
                which, m = divmod(j, KC)
                dve.wait_ge(diff_done, upto(s))
                v.scalar_tensor_tensor(out=mix32[:, j, :], in0=diff[:, m, :],
                                       scalar=chan[:, MIX_K + which, m:m + 1],
                                       in1=shifted[:, m, 0:T], op0=ALU.mult, op1=ALU.add)\
                    .then_inc(mix_done, 1)

            def mix_lo(s, j):
                dve.wait_ge(mix_hi_done, upto(s, 6, j))
                v.tensor_tensor(mix_l[:, j, :], mix32[:, j, :], mix_h[:, j, :], ALU.subtract)\
                    .then_inc(mix_lo_done, 1)

            def kv(s, m):
                dve.wait_ge(k_copied, upto(s, KC, m))
                dve.wait_ge(v_done, upto(s, KC, m))
                v.scalar_tensor_tensor(out=kv_sb[:, m, :], in0=ps[:, bank_of(s, "kv_proj", m, 1), :],
                                       scalar=W_UNSCALE, in1=k_sb[:, m, :], op0=ALU.mult,
                                       op1=ALU.mult).then_inc(kv_done, 1)

            def scan(s, m):
                dve.wait_ge(kv_done, upto(s, KC, m))
                v.tensor_tensor_scan(state[:, m, :], decay[:, m:m + 1].to_broadcast([P, T]),
                                     kv_sb[:, m, :], 0.0, ALU.mult, ALU.add).then_inc(scan_done, 1)

            def bonus(s, m):
                dve.wait_ge(scan_done, upto(s, KC, m))
                v.scalar_tensor_tensor(out=state[:, m, :], in0=kv_sb[:, m, :],
                                       scalar=chan[:, FIRST, m:m + 1], in1=state[:, m, :],
                                       op0=ALU.mult, op1=ALU.add).then_inc(bonus_done, 1)

            def receptance(s):
                dve.wait_ge(bonus_done, upto(s, KC, KC - 1))
                dve.wait_ge(r_copied, upto(s, KC, KC - 1))
                v.tensor_tensor(state, state, r_sb, ALU.mult).then_inc(mixed_done, 1)

            def o_lo(s, m):
                dve.wait_ge(o_hi_done, upto(s, KC, m))
                v.tensor_tensor(ol[:, m, :], o_aff[:, m, :], oh[:, m, :], ALU.subtract)\
                    .then_inc(o_lo_done, 1)

            def out_residual(s):
                for b in range(2):
                    dve.wait_ge(out_proj_done, upto(s, 2, b))
                    v.scalar_tensor_tensor(
                        out=x2_of(s)[:, 2 * b:2 * b + 2, :].rearrange("p j c -> p (j c)"),
                        in0=ps[:, bank_of(s, "out_proj", b), :], scalar=W_UNSCALE,
                        in1=x1[:, 2 * b:2 * b + 2, :].rearrange("p j c -> p (j c)"),
                        op0=ALU.mult, op1=ALU.add).then_inc(x2_done, 1)

            def top2(s, f):
                dve.wait_ge(router_done[f], upto(s))
                parts = ps[:, bank_of(s, "router", f, 0), 0:NT * 2 * NE]\
                    .rearrange("p (j h e) -> p j h e", j=NT, h=2)
                v.tensor_scalar(logits_lo[:], parts[:, :, 1, :], W_UNSCALE, None, ALU.mult)\
                    .then_inc(logits_lo_out[f], 1)
                dve.wait_ge(logits_lo_out[f], upto(s))
                v.scalar_tensor_tensor(out=logits[f][:], in0=parts[:, :, 0, :], scalar=W_UNSCALE,
                                       in1=logits_lo[:], op0=ALU.mult, op1=ALU.add)\
                    .then_inc(logits_out[f], 1)
                own_wait(dve, logits_out[f], upto(s))
                for j in range(NT):
                    ins = v.max(out=best[f][:, j, :], in_=logits[f][:, j, :])
                ins.then_inc(max_done[f], 1)
                own_wait(dve, max_done[f], upto(s))
                for j in range(NT):
                    ins = v.max_index(out=best_at[f][:, j, :], in_max=best[f][:, j, :],
                                      in_values=logits[f][:, j, :])
                ins.then_inc(top2_done[f], 1)

            def combine(s, f):
                all_ = [P, NT, TOPK, NE]
                dve.wait_ge(exp_done[f], upto(s))
                v.tensor_scalar(p_one[:], p_exp[f][:], 1.0, None, ALU.add).then_inc(comb_step[f], 1)
                v.tensor_tensor(chosen[:], experts[:],
                                best_at[f][:, :, 0:TOPK].unsqueeze(3).to_broadcast(all_),
                                ALU.is_equal).then_inc(comb_step[f], 1)
                dve.wait_ge(comb_step[f], upto(s, 8, 0))
                v.reciprocal(score[:], p_one[:]).then_inc(comb_step[f], 1)
                dve.wait_ge(comb_step[f], upto(s, 8, 2))
                v.tensor_tensor(score_sum[:], score[:, :, 0], score[:, :, 1], ALU.add)\
                    .then_inc(comb_step[f], 1)
                dve.wait_ge(comb_step[f], upto(s, 8, 3))
                v.tensor_scalar(score_eps[:], score_sum[:], 1e-20, None, ALU.add)\
                    .then_inc(comb_step[f], 1)
                dve.wait_ge(comb_step[f], upto(s, 8, 4))
                v.reciprocal(score_inv[:], score_eps[:]).then_inc(comb_step[f], 1)
                dve.wait_ge(comb_step[f], upto(s, 8, 5))
                v.scalar_tensor_tensor(out=share[:], in0=score[:], scalar=ROUTE_SCALE,
                                       in1=score_inv[:].unsqueeze(2).to_broadcast([P, NT, TOPK]),
                                       op0=ALU.mult, op1=ALU.mult).then_inc(comb_step[f], 1)
                dve.wait_ge(comb_step[f], upto(s, 8, 6))
                v.tensor_tensor(chosen_w[:], chosen[:],
                                share[:].unsqueeze(3).to_broadcast(all_), ALU.mult)\
                    .then_inc(comb_step[f], 1)
                dve.wait_ge(comb_step[f], upto(s, 8, 7))
                v.tensor_tensor(comb[:], chosen_w[:, :, 0, :], chosen_w[:, :, 1, :], ALU.add)\
                    .then_inc(comb_done[f], 1)

            for e in range(NE):
                last_set = v.memset(experts[:, :, :, e], float(e))
            last_set.then_inc(stored, 16)
            dve.wait_ge(consts, 2)
            walk(dve, tables["dve"], {
                "gated": gated, "weigh": weigh, "hidden_lo": hidden_lo, "residual": residual,
                "stats": stats, "norm": norm, "x_lo": x_lo, "shift_diff": shift_diff, "mix": mix,
                "mix_lo": mix_lo, "kv": kv, "scan": scan, "bonus": bonus, "receptance": receptance,
                "o_lo": o_lo, "out_residual": out_residual, "top2": top2, "combine": combine})


def kernel(**inputs):
    import numpy as np
    import concourse.bacc as bacc
    from concourse.bass_utils import run_bass_kernel_spmd

    a = {k: np.asarray(v) for k, v in inputs.items()}
    C = a["L0_attn_x"].shape[-1]
    KC = C // P

    def lhs(w):
        return w.T.reshape(KC, P, -1).transpose(1, 0, 2)

    chunks = []
    shared = a["L0_ffn_ws_gate"].shape[0] // P
    for c in range(shared):
        rows = slice(c * P, (c + 1) * P)
        chunks.append((a["L0_ffn_ws_gate"][rows], a["L0_ffn_ws_up"][rows],
                       a["L0_ffn_ws_down"][:, rows]))
    for e in range(a["L0_ffn_w_gate"].shape[0]):
        chunks.append((a["L0_ffn_w_gate"][e], a["L0_ffn_w_up"][e], a["L0_ffn_w_down"][e]))
    w_chunks = np.stack([
        np.concatenate([np.concatenate([lhs(g), lhs(u)], axis=2).reshape(P, -1), d.T], axis=1)
        for g, u, d in chunks])
    w_attn = np.stack([lhs(a[f"L0_attn_{n}"]) for n in ("Wk", "Wv", "Wr", "Wo")], axis=1)
    channels = np.stack([a[f"L0_attn_{n}"].reshape(KC, P).T for n in (
        "time_mix_k", "time_mix_v", "time_mix_r", "time_decay", "time_first", "ln_g", "ln_b")],
        axis=1)
    arrays = {"x": a["L0_attn_x"], "w_chunks": w_chunks, "w_attn": w_attn,
              "w_router": lhs(a["L0_ffn_gate_weight"]), "channels": channels}
    arrays = {f"in_{k}_dram": np.ascontiguousarray(v) for k, v in arrays.items()}

    nc = bacc.Bacc("TRN2", target_bir_lowering=False, num_devices=1)
    args = [nc.dram_tensor(k, v.shape, mybir.dt.from_np(v.dtype), kind="ExternalInput").ap()
            for k, v in arrays.items()]
    out = nc.dram_tensor("out_0_dram", a["L0_attn_x"].shape, F32, kind="ExternalOutput").ap()
    experts, tokens = a["L0_ffn_w_gate"].shape[0], a["L0_attn_x"].shape[1]
    comb_dram = {f: nc.dram_tensor(f"comb{f}", [experts, tokens], F32).ap() for f in "AB"}
    program(nc, *args, comb_dram, out)
    r = run_bass_kernel_spmd(nc, [arrays], core_ids=[0])
    return r.results[0]["out_0_dram"]
```
